# Optimizing a Trainium2 kernel written in Bass

```python
import numpy as np
import jax
import jax.numpy as jnp

def _softmax(x, axis=-1):
    return jax.nn.softmax(x, axis=axis)

def _gelu(x):
    return jax.nn.gelu(x, approximate=True)

def _silu(x):
    return jax.nn.silu(x)

def _sigmoid(x):
    return jax.nn.sigmoid(x)

def _layernorm(x, axis=-1, eps=1e-05):
    m = jnp.mean(x, axis=axis, keepdims=True)
    v = jnp.var(x, axis=axis, keepdims=True)
    return (x - m) / jnp.sqrt(v + eps)

def _scatter_add(tgt, idx, src, axis=0):
    return tgt.at[idx].add(src)

def _segment_sum(src, seg, n):
    return jax.ops.segment_sum(src, seg, n)
kernel_name = 'mk_flamingo_gated_d1_seqx_r8_325134'

def setup_inputs(seed: int=0):
    np.random.seed(seed)
    _w = jnp.asarray

    def _rec_inputs():
        import jax
        import jax.numpy as jnp
        _rk = jax.random.key(seed)
        x = -0.0002928 + 1 * jax.random.normal(jax.random.fold_in(_rk, 1), (16, 56, 128), jnp.float32)
        _lenS = 56 - jax.random.randint(jax.random.fold_in(_rk, 7), (16,), 0, max(1, 56 // 4) + 1, jnp.int32)
        _lenS2 = 1500 - jax.random.randint(jax.random.fold_in(_rk, 8), (16,), 0, max(1, 1500 // 4) + 1, jnp.int32)
        _ctx_1024P = jax.random.normal(jax.random.fold_in(_rk, 11), (16, 16, 128), jnp.float32)
        _ctx_1024c = jax.random.dirichlet(jax.random.fold_in(_rk, 511), 0.3 * jnp.ones((16,), jnp.float32), (16, 1500))
        _ctx_1024t = jnp.einsum('bsk,bkd->bsd', _ctx_1024c, _ctx_1024P)
        _ctx_1024t = _ctx_1024t * jax.lax.rsqrt(jnp.mean(jnp.square(_ctx_1024t)) + 1e-12) * 0.953939
        ctx_1024 = -1.39393e-06 + 0.999914 * (_ctx_1024t + 0.3 * jax.random.normal(jax.random.fold_in(_rk, 611), (16, 1500, 128), jnp.float32))
        _validS = jnp.arange(56)[None, :] < _lenS[:, None]
        _validS2 = jnp.arange(1500)[None, :] < _lenS2[:, None]
        _causal = jnp.tril(jnp.ones((56, 56), dtype=bool))
        mask_BxSxS2_if1 = jnp.where(jnp.ones((16, 56, 1500), dtype=bool), 1, 0).astype(jnp.int32)
        _g = jax.random.normal(jax.random.fold_in(_rk, 9001), (2, 1), jnp.float32)
        _g = jnp.sign(_g) * jnp.maximum(jnp.abs(_g), 1.0) + (_g == 0) * 1.0
        g_xattn = _g[0]
        g_ffn = _g[1]
        return (x, ctx_1024, mask_BxSxS2_if1, g_xattn, g_ffn)
    x, ctx_1024, mask_BxSxS2_if1, g_xattn, g_ffn = _rec_inputs()

    def _L0_xattn_setup():
        import jax, jax.numpy as jnp
        import numpy as np
        B, S, D, H = (2, 256, 128, 16)
        DH = D // H
        key = jax.random.key(seed)
        ks = jax.random.split(key, 12)
        sc = 0.02
        return {'query': jax.random.normal(ks[0], (B, S, D), jnp.float32), 'key': jax.random.normal(ks[1], (B, S, D), jnp.float32), 'value': jax.random.normal(ks[2], (B, S, D), jnp.float32), 'mask': jnp.ones((B, S, S), jnp.int32), 'qw': jax.random.normal(ks[3], (D, D), jnp.float32) * sc, 'qb': jnp.zeros((D,), jnp.float32), 'kw': jax.random.normal(ks[4], (D, D), jnp.float32) * sc, 'kb': jnp.zeros((D,), jnp.float32), 'vw': jax.random.normal(ks[5], (D, D), jnp.float32) * sc, 'vb': jnp.zeros((D,), jnp.float32), 'ow': jax.random.normal(ks[6], (D, D), jnp.float32) * sc, 'ob': jnp.zeros((D,), jnp.float32)}
    _L0_xattn_all = _L0_xattn_setup()
    _L0_xattn_in = {k: v for k, v in _L0_xattn_all.items() if k in ('qw', 'qb', 'kw', 'kb', 'vw', 'vb', 'ow', 'ob')}
    del _L0_xattn_all

    def _L0_ffn_setup():
        import jax, jax.numpy as jnp
        import numpy as np
        H = 128
        I = 4 * H
        E = 8
        K = 2
        B, S = (2, 128)
        STD = 0.02 / np.sqrt(H)
        key = jax.random.key(seed)
        ks = jax.random.split(key, 8)
        x = jax.random.normal(ks[0], (B, S, H), dtype=jnp.float32)
        gate_w = jax.random.normal(ks[1], (H, E), dtype=jnp.float32) * STD
        bias = jnp.zeros((E,), dtype=jnp.float32)
        up_w = jax.random.normal(ks[2], (E, H, I), dtype=jnp.float32) * STD
        up_b = jnp.zeros((E, I), dtype=jnp.float32)
        down_w = jax.random.normal(ks[3], (E, I, H), dtype=jnp.float32) * STD
        down_b = jnp.zeros((E, H), dtype=jnp.float32)
        sw_up = jax.random.normal(ks[4], (H, I), dtype=jnp.float32) * STD
        sb_up = jnp.zeros((I,), dtype=jnp.float32)
        sw_down = jax.random.normal(ks[5], (I, H), dtype=jnp.float32) * STD
        sb_down = jnp.zeros((H,), dtype=jnp.float32)
        return {'x': x, 'gate_w': gate_w, 'bias': bias, 'up_w': up_w, 'up_b': up_b, 'down_w': down_w, 'down_b': down_b, 'sw_up': sw_up, 'sb_up': sb_up, 'sw_down': sw_down, 'sb_down': sb_down}
    _L0_ffn_all = _L0_ffn_setup()
    _L0_ffn_in = {k: v for k, v in _L0_ffn_all.items() if k in ('gate_w', 'bias', 'up_w', 'up_b', 'down_w', 'down_b', 'sw_up', 'sb_up', 'sw_down', 'sb_down')}
    del _L0_ffn_all
    return {'x': x, 'ctx_1024': ctx_1024, 'mask_BxSxS2_if1': mask_BxSxS2_if1, 'g_xattn': g_xattn, 'g_ffn': g_ffn, 'L0_xattn_qw': _L0_xattn_in['qw'], 'L0_xattn_qb': _L0_xattn_in['qb'], 'L0_xattn_kw': _L0_xattn_in['kw'], 'L0_xattn_kb': _L0_xattn_in['kb'], 'L0_xattn_vw': _L0_xattn_in['vw'], 'L0_xattn_vb': _L0_xattn_in['vb'], 'L0_xattn_ow': _L0_xattn_in['ow'], 'L0_xattn_ob': _L0_xattn_in['ob'], 'L0_ffn_gate_w': _L0_ffn_in['gate_w'], 'L0_ffn_bias': _L0_ffn_in['bias'], 'L0_ffn_up_w': _L0_ffn_in['up_w'], 'L0_ffn_up_b': _L0_ffn_in['up_b'], 'L0_ffn_down_w': _L0_ffn_in['down_w'], 'L0_ffn_down_b': _L0_ffn_in['down_b'], 'L0_ffn_sw_up': _L0_ffn_in['sw_up'], 'L0_ffn_sb_up': _L0_ffn_in['sb_up'], 'L0_ffn_sw_down': _L0_ffn_in['sw_down'], 'L0_ffn_sb_down': _L0_ffn_in['sb_down']}

def reference(x, ctx_1024, mask_BxSxS2_if1, g_xattn, g_ffn, L0_xattn_qw, L0_xattn_qb, L0_xattn_kw, L0_xattn_kb, L0_xattn_vw, L0_xattn_vb, L0_xattn_ow, L0_xattn_ob, L0_ffn_gate_w, L0_ffn_bias, L0_ffn_up_w, L0_ffn_up_b, L0_ffn_down_w, L0_ffn_down_b, L0_ffn_sw_up, L0_ffn_sb_up, L0_ffn_sw_down, L0_ffn_sb_down):
    import jax
    import jax.numpy as jnp

    def _L0_xattn_ref(query, key, value, mask, qw, qb, kw, kb, vw, vb, ow, ob):
        import jax, jax.numpy as jnp
        import numpy as np
        B, S, D, H = (2, 256, 128, 16)
        DH = D // H
        q = query @ qw.T + qb
        k = key @ kw.T + kb
        v = value @ vw.T + vb

        def split(x):
            b, s, _ = x.shape
            return x.reshape(b, s, H, DH).transpose(0, 2, 1, 3)
        qh, kh, vh = (split(q), split(k), split(v))
        scale = DH ** (-0.5)
        scores = jnp.einsum('bhqd,bhkd->bhqk', qh * scale, kh)
        scores = jnp.where(mask[:, None] == 0, jnp.float32(-1000000000.0), scores)
        probs = jax.nn.softmax(scores, axis=-1)
        out = jnp.einsum('bhqk,bhkd->bhqd', probs, vh)
        out = out.transpose(0, 2, 1, 3).reshape(out.shape[0], -1, H * DH)
        return out @ ow.T + ob

    def _L0_ffn_ref(x, gate_w, bias, up_w, up_b, down_w, down_b, sw_up, sb_up, sw_down, sb_down):
        import jax, jax.numpy as jnp
        import numpy as np
        H = 128
        I = 4 * H
        E = 8
        K = 2
        B, S = (2, 128)
        STD = 0.02 / np.sqrt(H)
        b, s, h = x.shape
        xf = x.reshape(-1, h)
        T = xf.shape[0]
        scores = jax.nn.sigmoid(xf @ gate_w + bias)
        top_scores, top_idx = jax.lax.top_k(scores, K)
        top_scores = top_scores / (jnp.sum(top_scores, axis=-1, keepdims=True) + 1e-06)
        w = jnp.zeros((T, E), dtype=xf.dtype).at[jnp.arange(T)[:, None], top_idx].add(top_scores)
        up = jnp.einsum('th,ehi->tei', xf, up_w) + up_b
        hact = jax.nn.gelu(up, approximate=False)
        eo = jnp.einsum('tei,eih->teh', hact, down_w) + down_b
        combined = jnp.einsum('teh,te->th', eo * 0.1, w)
        shared = (jax.nn.gelu(xf @ sw_up + sb_up, approximate=False) @ sw_down + sb_down) * 0.1
        out = (shared + combined).reshape(b, s, h)
        out = out / (jnp.max(jnp.abs(out), axis=-1, keepdims=True) + 1e-06)
        return out
    x = x + jnp.tanh(g_xattn[0]) * _L0_xattn_ref(_layernorm(x, axis=-1), ctx_1024, ctx_1024, mask_BxSxS2_if1, L0_xattn_qw, L0_xattn_qb, L0_xattn_kw, L0_xattn_kb, L0_xattn_vw, L0_xattn_vb, L0_xattn_ow, L0_xattn_ob)
    x = x + jnp.tanh(g_ffn[0]) * _L0_ffn_ref(_layernorm(x, axis=-1), L0_ffn_gate_w, L0_ffn_bias, L0_ffn_up_w, L0_ffn_up_b, L0_ffn_down_w, L0_ffn_down_b, L0_ffn_sw_up, L0_ffn_sb_up, L0_ffn_sw_down, L0_ffn_sb_down)
    return x

_drawn_inputs = setup_inputs


def setup_inputs(seed=0):
    import zlib

    import numpy as np

    out = dict(_drawn_inputs(seed))
    spreads = {'L0_xattn_qb': (0.0, 2.0),
     'L0_xattn_kb': (0.0, 2.0),
     'L0_xattn_vb': (0.0, 0.385),
     'L0_xattn_ob': (0.0, 0.1),
     'L0_ffn_bias': (0.0, 0.1),
     'L0_ffn_up_b': (0.0, 0.8),
     'L0_ffn_down_b': (0.0, 0.1),
     'L0_ffn_sb_up': (0.0, 0.8),
     'L0_ffn_sb_down': (0.0, 0.1)}
    factors = {'L0_xattn_qw': 8.0,
     'L0_xattn_kw': 8.0,
     'L0_ffn_up_w': 8.0,
     'L0_ffn_down_w': 8.0,
     'L0_ffn_sw_up': 8.0,
     'L0_ffn_sw_down': 7.684}
    for name, (base, spread) in spreads.items():
        noise = np.random.default_rng([zlib.crc32(name.encode()), seed]).standard_normal(out[name].shape)
        drawn = base * np.exp(spread * noise) if base else spread * noise
        out[name] = jnp.asarray(drawn.astype(out[name].dtype))
    for name, factor in factors.items():
        out[name] = (out[name] * factor).astype(out[name].dtype)
    return out
```

```python
from contextlib import ExitStack

import numpy as np
import concourse.bass as bass
from concourse import mybir

ALU = mybir.AluOpType
ACT = mybir.ActivationFunctionType
F32 = mybir.dt.float32
F16 = mybir.dt.float16
I32 = mybir.dt.int32
AX = mybir.AxisListType

P = 128
B, S, D, H = 16, 56, 128, 16
DH = D // H
NK = 1500
KT = 12
KLAST = NK - (KT - 1) * P
PAIRS = H // 2
QW = 2 * S
HQ = H * S
RT = HQ // P
TOK = B * S
TT = TOK // P
MROW = 64
ONEROW = MROW + S
NCH = 3
CH = NK // NCH
VW = DH + 1
WIN = 4
H0 = [min(P * t // S, H - WIN) for t in range(RT)]
BIG = 32768.0
E = 8
NE = E + 1
HID = 4 * D
HC = HID // P
EPS = 1e-5
HALF = TOK // 2


def constants():
    row = np.arange(HQ).reshape(RT, P)
    head, query = row // S, row % S
    pick = (query[:, :, None] == np.arange(S)).transpose(1, 0, 2).astype(np.float32)
    own = (head[:, :, None] == (np.array(H0)[:, None] + np.arange(WIN))[:, None, :])
    own = np.repeat(own.transpose(1, 0, 2)[..., None], DH, axis=3).reshape(P, RT, WIN * DH)
    onehot = np.tile(np.eye(S, dtype=np.float16) * np.float16(BIG), (1, 2 * PAIRS))
    parity = ((np.arange(4 * 2 * DH) // DH % 2)[:, None] == np.arange(2)).astype(np.float32)
    parity = np.concatenate([parity, parity * (np.arange(64) >= 32)[:, None]], axis=1).astype(np.float32)
    rank = np.tile(np.arange(E, 0, -1, dtype=np.float32), (P, TT))
    return {
        "c_ident": np.eye(P, dtype=np.float32),
        "c_pick": pick,
        "c_own": own.astype(np.float32),
        "c_onehot": onehot,
        "c_parity": parity,
        "c_rank": rank,
    }


def flamingo_kernel(nc, d, out):
    with ExitStack() as ctx:
        def sb(name, shape, dt=F32):
            return ctx.enter_context(nc.sbuf_tensor(name, shape, dt))

        def sem(name):
            return ctx.enter_context(nc.semaphore(name))

        ident = sb("ident", [P, P])
        pick = sb("pick", [P, RT, S])
        own = sb("own", [P, RT, WIN * DH])
        onehot = sb("onehot", [P, PAIRS * QW], F16)
        parity = sb("parity", [64, 4])
        rank = sb("rank", [P, TT * E])
        w_raw = sb("w_raw", [P, 4, D])
        w_t = sb("w_t", [P, 4, D])
        q_bias = sb("q_bias", [P, D])
        k_bias = sb("k_bias", [P, 1])
        v_bias = sb("v_bias", [P, 1])
        gates = sb("gates", [P, 2])
        tanh_g = sb("tanh_g", [P, 2])
        xq = sb("xq", [P, B, D])
        stat = sb("stat", [P, B, 6])
        mv = sb("mv", [P, B, 2])
        rstd = sb("rstd", [P, B])
        lnT = sb("lnT", [P, B * S])
        q_all = sb("q_all", [P, B, D])
        q_any = sb("q_any", [P, PAIRS, 4, 16])
        q_rows = sb("q_rows", [64, PAIRS, S])
        q_val = sb("q_val", [64, PAIRS, S])
        q_hi = sb("q_hi", [64, PAIRS, S], F16)
        mask_raw = sb("mask_raw", [P, 2, NK], I32)
        mask_abs = sb("mask_abs", [P, 1])
        any_key = sb("any_key", [P, 1])
        fill = sb("fill", [P, 1])
        mask_add = sb("mask_add", [P, NK], F16)
        ctx_raw = sb("ctx_raw", [P, 2, KT, D])
        ctxT = sb("ctxT", [P, NK])
        k_hi = sb("k_hi", [P, NK], F16)
        k_lo = sb("k_lo", [P, NK], F16)
        keys = sb("keys", [P, 2, PAIRS, NK], F16)
        qrs = sb("qrs", [P, 2, PAIRS, 2, S], F16)
        v_ext = sb("v_ext", [P, 2, KT, H, VW])
        max_part = sb("max_part", [QW, PAIRS, NCH])
        neg_max = sb("neg_max", [QW, PAIRS])
        max_rows = sb("max_rows", [PAIRS, QW], F16)
        probs = sb("probs", [P, 3, HQ])
        recip = sb("recip", [P, RT])
        normed = sb("normed", [P, RT, WIN * DH])
        blocks = sb("blocks", [P, RT, D])
        attnT = sb("attnT", [P, TOK])

        x_tok = sb("x_tok", [P, TT, D])
        o_bias = sb("o_bias", [P, D])
        gate_w = sb("gate_w", [P, E])
        gate_b = sb("gate_b", [P, E])
        up_b_raw = sb("up_b_raw", [NE * HC, P])
        up_bias = sb("up_bias", [P, NE * HC])
        down_b = sb("down_b", [NE, D])
        up_w = sb("up_w", [P, 2, HID])
        down_w = sb("down_w", [P, 2, HC, D])
        ln_stat = sb("ln_stat", [P, TT, 6])
        ln_mv = sb("ln_mv", [P, TT, 2])
        ln_rstd = sb("ln_rstd", [P, TT])
        xn = sb("xn", [P, TT, D])
        xnT = lnT
        score = sb("score", [P, TT, E])
        topv = sb("topv", [P, 2, TT])
        pick1 = sb("pick1", [P, TT, E])
        pick2 = sb("pick2", [P, TT, E])
        tmp = sb("tmp", [P, TT, E])
        tmpv = sb("tmpv", [P, TT])
        route = sb("route", [P, NE, TT])
        routeT = sb("routeT", [NE, TOK])
        acc = sb("acc", [P, TT, D])
        hidden = keys[:, :, :, :].rearrange("p u a k -> p (u a k)").bitcast(F32)[:, 0:2 * HC * TOK]\
            .rearrange("p (u c t) -> p u c t", u=2, c=HC)

        ring = ctx.enter_context(nc.psum_tensor("ring", [P, 3, 512], F32))
        st = ctx.enter_context(nc.psum_tensor("st", [P, 2, 2, 512], F32))
        pv = ctx.enter_context(nc.psum_tensor("pv", [P, 512], F32))
        pv_win = pv[:, 0:RT * WIN * VW].rearrange("p (t h w) -> p t h w", t=RT, h=WIN)

        names = """
        consts_loaded weights_loaded qrow_loaded x_loaded mask_placed max_placed
        ones_set
        w_turned w_copied stats_done rstd_var rstd_done ln_done ln_turned ln_copied q_made q_stored
        ctx_turned ctx_copied k_made k_hi_stored k_lo_stored v_made v_stored
        mask_abs_done any_done mask_ready onehot_placed q_blanked q_spread q_copied q_step blocks_zeroed
        scored max_read max_merged max_turned max_copied
        st_made exps_done pv_done recip_done normed_done blocks_done attn_made attn_stored dve_step
        ffn_consts gates_tanh projected x1_step x1_done ffn_var ffn_ln_done xn_turned xn_copied bias_turned
        bias_copied gate_made score_raw score_done route_step route_done route_turned route_copied
        bias_mixed acc_ready up_made hidden_done down_made mixed out_step out_ready out_stored
        """.split()
        s = {n: sem("s_" + n) for n in names}
        ctx_loaded = [sem(f"s_ctx_loaded{u}") for u in range(2)]
        mask_loaded = [sem(f"s_mask_loaded{u}") for u in range(2)]
        expert_loaded = [sem(f"s_expert_loaded{u}") for u in range(2)]

        def turn(k, u):
            return k - u + 2

        rows_placed = [sem(f"s_rows_placed{p}") for p in range(PAIRS)]

        block = ctx.enter_context(nc.Block())

        def tile_keys(j):
            return P if j < KT - 1 else KLAST

        mr = slice(MROW, MROW + S)


        def sp_load_batch(sp, n):
            u = n[1]
            k = n[0]
            src = d["ctx"][bass.ds(k, 1), :, :]
            sp.dma_start(ctx_raw[:, u, 0:KT - 1, :],
                         src[:, 0:(KT - 1) * P, :].rearrange("b (t p) d -> p (b t) d", p=P)).then_inc(ctx_loaded[u], 16)
            sp.dma_start(ctx_raw[0:KLAST, u, KT - 1, :],
                         src[:, (KT - 1) * P:NK, :].rearrange("b p d -> p (b d)")).then_inc(ctx_loaded[u], 16)
            sp.dma_start(mask_raw[mr, u, :],
                         d["mask"][bass.ds(k, 1), :, :].rearrange("b q k -> q (b k)")).then_inc(mask_loaded[u], 16)

        def sp_place(sp, n):
            k, u = n
            sp.wait_ge(s["mask_ready"], k + 1)
            sp.dma_start(keys[mr, u, :, :],
                         mask_add[mr, :].unsqueeze(1).to_broadcast([S, PAIRS, NK])).then_inc(s["mask_placed"], 16)
            sp.wait_ge(s["k_lo_stored"], NCH * (k + 1))
            for p in range(PAIRS):
                for r in range(4):
                    part = k_hi if r % 2 == 0 else k_lo
                    sp.dma_start(keys[16 * r:16 * r + 16, u, p, :],
                                 part[16 * p:16 * p + 16, :]).then_inc(rows_placed[p], 16)

        def sp_place_max(sp, n):
            k, u = n
            sp.wait_ge(s["max_copied"], k + 1)
            for p in range(PAIRS):
                sp.dma_start(qrs[ONEROW:ONEROW + 1, u, p, :, :].rearrange("r h q -> r (h q)"),
                             max_rows[p:p + 1, :]).then_inc(s["max_placed"], 16)

        def pe_ctx_turn(pe, n, c):
            k, u = n
            if c == 0:
                pe.wait_ge(ctx_loaded[u], 16 * turn(k, u))
            ring_free(pe, n, ("T", c))
            for i in range(4):
                j = 4 * c + i
                m = tile_keys(j)
                mm = nc.tensor.transpose(ring[:, RING[("T", c)], i * P:i * P + m],
                                         ctx_raw[0:m, u, j, :], ident[0:m, 0:m])
            mm.then_inc(s["ctx_turned"], 1)

        def pe_k(pe, n, c):
            k, u = n
            ring_free(pe, n, ("K", c))
            if c == 0:
                pe.wait_ge(s["ctx_copied"], NCH * (k + 1))
            nc.tensor.matmul(ring[:, RING[("K", c)], 0:CH], w_t[:, 1, :], ctxT[:, c * CH:(c + 1) * CH],
                             start=True, stop=True).then_inc(s["k_made"], 1)

        def pe_v(pe, n, c):
            ring_free(pe, n, ("V", c))
            if c == 0:
                ring_free(pe, n, ("Q", 0))
                pe.wait_ge(s["q_blanked"], n[0] + 1)
            for i in range(4):
                j = 4 * c + i
                m = tile_keys(j)
                mm = nc.tensor.matmul(ring[0:m, RING[("V", c)], i * P:(i + 1) * P], ctxT[:, j * P:j * P + m],
                                      w_t[:, 2, :], start=True, stop=True)
            mm.then_inc(s["v_made"], 1)

        def pe_q(pe, n):
            k, u = n
            bank = ring[0:64, RING[("Q", 0)], 0:PAIRS * S].rearrange("r (p q) -> r p q", p=PAIRS)
            for p in range(PAIRS):
                mm = nc.tensor.matmul(bank[:, p, :],
                                      q_any[mr, p, :, :].rearrange("q r d -> q (r d)"),
                                      ident[mr, mr], start=True, stop=True)
            mm.then_inc(s["q_spread"], 1)

        def pe_score(pe, n, m):
            k, u = n
            p, c = divmod(m, NCH)
            if m == 0:
                pe.wait_ge(s["mask_placed"], 16 * (k + 1))
                pe.wait_ge(s["onehot_placed"], k + 1)
                pe.wait_ge(s["q_step"], 4 * (k + 1))
            if c == 0:
                pe.wait_ge(rows_placed[p], 64 * (k + 1))
            ring_free(pe, n, ("S", m))
            nc.tensor.matmul(ring[0:QW, RING[("S", m)], 0:CH],
                             qrs[0:ONEROW, u, p, :, :].rearrange("r h q -> r (h q)"),
                             keys[0:ONEROW, u, p, c * CH:(c + 1) * CH],
                             start=True, stop=True).then_inc(s["scored"], 1)

        def pe_max_turn(pe, n):
            k, u = n
            ring_free(pe, n, ("M", 0))
            pe.wait_ge(s["max_merged"], k + 1)
            nc.tensor.transpose(ring[0:PAIRS, RING[("M", 0)], 0:QW], neg_max[:, :],
                                ident[0:QW, 0:QW]).then_inc(s["max_turned"], 1)

        def pe_scores_t(pe, b, j):
            k, u = b
            m = tile_keys(j)
            if j == 0:
                pe.wait_ge(s["max_placed"], 16 * PAIRS * (k + 1))
            if j >= 2:
                pe.wait_ge(s["exps_done"], KT * k + j - 1)
            elif isinstance(k, int) is False or k > 0:
                pe.wait_ge(s["exps_done"], KT * k + j - 1)
            for p in range(PAIRS):
                mm = nc.tensor.matmul(st[0:m, j % 2, p // 4, QW * (p % 4):QW * (p % 4 + 1)],
                                      keys[0:ONEROW + 1, u, p, j * P:j * P + m],
                                      qrs[0:ONEROW + 1, u, p, :, :].rearrange("r h q -> r (h q)"),
                                      start=True, stop=True)
            mm.then_inc(s["st_made"], 1)

        def pe_pv(pe, b, j):
            k, u = b
            m = tile_keys(j)
            pe.wait_ge(s["exps_done"], KT * k + j + 1)
            if j == 0:
                pe.wait_ge(s["v_stored"], NCH * (k + 1))
                if not (isinstance(k, int) and k == 0):
                    pe.wait_ge(s["normed_done"], k)
            for t in range(RT):
                mm = nc.tensor.matmul(pv_win[:, t, :, :].rearrange("p h w -> p (h w)"),
                                      probs[0:m, j % 3, t * P:(t + 1) * P],
                                      v_ext[0:m, u, j, H0[t]:H0[t] + WIN, :].rearrange("p h w -> p (h w)"),
                                      start=(j == 0 and t == 0), stop=(j == KT - 1), skip_group_check=True)
            mm.then_inc(s["pv_done"], 1)

        def pe_attn(pe, b):
            k, u = b
            if isinstance(k, int) and k >= B - 2:
                pe.wait_ge(s["max_copied"], B)
                pe.wait_ge(s["max_read"], PAIRS * NCH * B)
                pe.wait_ge(s["attn_stored"], k)
            else:
                ring_free(pe, (k + 2, u), ("A", 0))
            pe.wait_ge(s["blocks_done"], k + 1)
            for t in range(RT):
                mm = nc.tensor.matmul(ring[:, RING[("A", 0)], 0:S], blocks[:, t, :], pick[:, t, :],
                                      start=(t == 0), stop=(t == RT - 1))
            mm.then_inc(s["attn_made"], 1)

        STEPS = [[("T", 0), ("T", 1), ("T", 2)],
                 [("K", 0), ("K", 1), ("K", 2)],
                 [("A", 0), ("V", 0), ("Q", 0)],
                 [("V", 1), ("V", 2)],
                 []]
        order = [x for st_ in STEPS for x in st_]
        per = [4, 4, 4, 3, 3, 3, 3]
        m = 0
        for q in per:
            STEPS.append([("S", m + i) for i in range(q)])
            m += q
        order += [("S", i) for i in range(PAIRS * NCH)] + [("M", 0)]
        assert len(order) % 3 == 0
        RING = {x: i % 3 for i, x in enumerate(order)}
        release = {"T": ("ctx_copied", NCH), "K": ("k_lo_stored", NCH), "V": ("v_stored", NCH),
                   "Q": ("q_copied", 1), "S": ("max_read", PAIRS * NCH), "M": ("max_copied", 1)}

        def ring_free(pe, n, slot):
            k, u = n[0], n[1]
            i = order.index(slot)
            prev = order[i - 3]
            if prev[0] == "A":
                if not (isinstance(k, int) and k <= 1):
                    pe.wait_ge(s["attn_stored"], k - 1)
                prev = order[i - 6]
                i -= 3
            name, count = release[prev[0]]
            if i >= 3:
                pe.wait_ge(s[name], count * k + prev[1] + 1)
            elif not (isinstance(k, int) and k == 0):
                pe.wait_ge(s[name], count * (k - 1) + prev[1] + 1)

        def pe_slot(pe, n, slot, attn_of=None):
            kind, c = slot
            if kind == "T":
                pe_ctx_turn(pe, n, c)
            elif kind == "K":
                pe_k(pe, n, c)
            elif kind == "V":
                pe_v(pe, n, c)
            elif kind == "Q":
                pe_q(pe, n)
            elif kind == "S":
                pe_score(pe, n, c)
            elif kind == "M":
                pe_max_turn(pe, n)
            elif attn_of is not None:
                pe_attn(pe, attn_of)

        def pe_unit(pe, b, prep, attn):
            for j in range(KT):
                for slot in STEPS[j]:
                    if slot[0] == "A":
                        if attn is not None:
                            pe_slot(pe, None, slot, attn)
                    elif prep is not None:
                        pe_slot(pe, prep, slot)
                if b is not None:
                    pe_scores_t(pe, b, j)
                    if j > 0:
                        pe_pv(pe, b, j - 1)
            if b is not None:
                pe_pv(pe, b, KT - 1)
            if prep is not None:
                pe_max_turn(pe, prep)

        def act_query(act, n):
            k, u = n
            act.wait_ge(s["any_done"], 2 * (k + 1))
            if not (isinstance(k, int) and k == 0):
                act.wait_ge(s["q_spread"], k)
            nc.scalar.activation(q_any[mr, :, :, :],
                                 q_all[mr, bass.ds(k, 1), :].rearrange("q b (p d) -> q (b p) d", p=PAIRS)
                                 .unsqueeze(2).to_broadcast([S, PAIRS, 4, 16]),
                                 ACT.Copy, scale=any_key[mr, 0:1]).then_inc(s["q_blanked"], 1)

        def act_slot(act, n, slot, attn=None):
            kind, c = slot
            if kind == "T":
                k, u = n
                act.wait_ge(s["ctx_turned"], NCH * k + c + 1)
                if c == 0 and not (isinstance(k, int) and k == 0):
                    act.wait_ge(s["v_made"], NCH * k)
                w = min(512, NK - 512 * c)
                nc.scalar.activation(ctxT[:, 512 * c:512 * c + w], ring[:, RING[slot], 0:w],
                                     ACT.Copy).then_inc(s["ctx_copied"], 1)
            elif kind == "K":
                k, u = n
                act.wait_ge(s["k_made"], NCH * k + c + 1)
                if c == 0 and not (isinstance(k, int) and k == 0):
                    for p in range(PAIRS):
                        act.wait_ge(rows_placed[p], 64 * k)
                nc.scalar.activation(k_hi[:, c * CH:(c + 1) * CH], ring[:, RING[slot], 0:CH], ACT.Identity,
                                     bias=k_bias[:, 0:1]).then_inc(s["k_hi_stored"], 1)
            elif kind == "V":
                k, u = n
                act.wait_ge(s["v_made"], NCH * k + c + 1)
                if c == 0 and not (isinstance(k, int) and k <= 1):
                    act.wait_ge(s["pv_done"], KT * (k - 1))
                full = 4 if c < NCH - 1 else 3
                src = ring[:, RING[slot], :].rearrange("p (i h w) -> p i h w", i=4, h=H)
                if c == NCH - 1:
                    nc.scalar.activation(v_ext[0:KLAST, u, KT - 1, :, 0:DH], src[0:KLAST, 3], ACT.Copy)
                nc.scalar.activation(v_ext[:, u, 4 * c:4 * c + full, :, 0:DH], src[:, 0:full],
                                     ACT.Copy).then_inc(s["v_stored"], 1)
            elif kind == "Q":
                k, u = n
                act.wait_ge(s["q_spread"], k + 1)
                if not (isinstance(k, int) and k == 0):
                    act.wait_ge(s["q_step"], 4 * k)
                nc.scalar.activation(q_rows[:, :, :].rearrange("r p q -> r (p q)"),
                                     ring[0:64, RING[slot], 0:PAIRS * S], ACT.Copy).then_inc(s["q_copied"], 1)
            elif kind == "A":
                k, u = attn
                act.wait_ge(s["attn_made"], k + 1)
                nc.scalar.activation(attnT[:, bass.ds(k * S, S)], ring[:, RING[slot], 0:S], ACT.Identity,
                                     bias=v_bias[:, 0:1]).then_inc(s["attn_stored"], 1)

        def act_exp(act, b, j):
            k, u = b
            m = tile_keys(j)
            act.wait_ge(s["st_made"], KT * k + j + 1)
            if j >= 3 or not (isinstance(k, int) and k == 0):
                act.wait_ge(s["pv_done"], KT * k + j - 2)
            nc.scalar.activation(probs[0:m, j % 3, :].rearrange("p (h c) -> p h c", h=2),
                                 st[0:m, j % 2, :, 0:HQ // 2], ACT.Exp).then_inc(s["exps_done"], 1)

        def act_unit(act, b, prep, attn):
            for j in range(KT):
                for slot in STEPS[j]:
                    if slot[0] == "A":
                        if attn is not None:
                            act_slot(act, None, slot, attn)
                    elif slot[0] in "TKVQ" and prep is not None:
                        act_slot(act, prep, slot)
                if prep is not None and j == 1:
                    act_query(act, prep)
                if b is not None:
                    act_exp(act, b, j)
            if prep is not None:
                k, u = prep
                act.wait_ge(s["max_turned"], k + 1)
                if not (isinstance(k, int) and k == 0):
                    act.wait_ge(s["max_placed"], 16 * PAIRS * k)
                nc.scalar.activation(max_rows[:, :], ring[0:PAIRS, RING[("M", 0)], 0:QW],
                                     ACT.Copy).then_inc(s["max_copied"], 1)

        def dve_mask(dve, n):
            k, u = n
            dve.wait_ge(mask_loaded[u], 8 * turn(k, u))
            if not (isinstance(k, int) and k == 0):
                dve.wait_ge(s["any_done"], 2 * k)
            nc.vector.tensor_reduce(mask_abs[mr, :], mask_raw[mr, u, :], AX.X, ALU.max,
                                    apply_absolute_value=True).then_inc(s["mask_abs_done"], 1)
            dve.wait_ge(s["mask_abs_done"], k + 1)
            if not (isinstance(k, int) and k == 0):
                dve.wait_ge(s["q_blanked"], k)
                dve.wait_ge(s["onehot_placed"], k)
            nc.vector.tensor_scalar(any_key[mr, :], mask_abs[mr, :], 0.0, None,
                                    ALU.is_gt).then_inc(s["any_done"], 1)
            dve.wait_ge(s["any_done"], 2 * k + 1)
            nc.vector.tensor_scalar(fill[mr, :], any_key[mr, :], -BIG, None, ALU.mult).then_inc(s["any_done"], 1)
            dve.wait_ge(s["any_done"], 2 * k + 2)
            if not (isinstance(k, int) and k == 0):
                dve.wait_ge(s["mask_placed"], 16 * k)
            nc.vector.tensor_scalar(mask_add[mr, :], mask_raw[mr, u, :], 0.0, fill[mr, 0:1],
                                    ALU.is_equal, ALU.mult).then_inc(s["mask_ready"], 1)

        def dve_k_lo(dve, n, c):
            k, u = n
            dve.wait_ge(s["k_hi_stored"], NCH * k + c + 1)
            nc.vector.scalar_tensor_tensor(out=k_lo[:, c * CH:(c + 1) * CH], in0=ring[:, RING[("K", c)], 0:CH],
                                           scalar=k_bias[:, 0:1], in1=k_hi[:, c * CH:(c + 1) * CH],
                                           op0=ALU.add, op1=ALU.subtract).then_inc(s["k_lo_stored"], 1)

        def dve_max(dve, n, m):
            k, u = n
            p, c = divmod(m, NCH)
            dve.wait_ge(s["scored"], PAIRS * NCH * k + m + 1)
            nc.vector.tensor_reduce(max_part[:, p, c:c + 1], ring[0:QW, RING[("S", m)], 0:CH], AX.X,
                                    ALU.max).then_inc(s["max_read"], 1)

        def dve_norm(dve, b):
            k, u = b
            dve.wait_ge(s["pv_done"], KT * (k + 1))
            nc.vector.reciprocal(recip[:, :], pv_win[:, :, WIN - 1, DH:VW]).then_inc(s["recip_done"], 1)
            dve.wait_ge(s["recip_done"], k + 1)
            if not (isinstance(k, int) and k == 0):
                dve.wait_ge(s["blocks_done"], k)
            nc.vector.tensor_tensor(normed[:, :, :].rearrange("p t (h w) -> p t h w", h=WIN),
                                    pv_win[:, :, :, 0:DH],
                                    recip[:, :].unsqueeze(2).unsqueeze(3).to_broadcast([P, RT, WIN, DH]),
                                    ALU.mult).then_inc(s["normed_done"], 1)

        def dve_unit(dve, b, prep, attn):
            if attn is not None:
                dve_norm(dve, attn)
            if prep is not None:
                dve_mask(dve, prep)
            if prep is not None:
                for c in range(NCH):
                    dve_k_lo(dve, prep, c)
                for m in range(PAIRS * NCH):
                    dve_max(dve, prep, m)
                k, u = prep
                dve.wait_ge(s["max_read"], PAIRS * NCH * (k + 1))
                if not (isinstance(k, int) and k == 0):
                    dve.wait_ge(s["max_turned"], k)
                nc.vector.tensor_reduce(neg_max[:, :], max_part[:, :, :], AX.X, ALU.max,
                                        negate=True).then_inc(s["max_merged"], 1)

        def pool_blocks(pool, b):
            k, u = b
            pool.wait_ge(s["normed_done"], k + 1)
            if not (isinstance(k, int) and k == 0):
                pool.wait_ge(s["attn_made"], k)
            for t in range(RT):
                op = nc.gpsimd.tensor_tensor(blocks[:, t, DH * H0[t]:DH * (H0[t] + WIN)], normed[:, t, :],
                                             own[:, t, :], ALU.mult)
            op.then_inc(s["blocks_done"], 1)

        def pool_unit(pool, b, prep, attn):
            if attn is not None:
                pool_blocks(pool, attn)
            if prep is not None:
                pool_onehot(pool, prep)
                pool_query(pool, prep)

        def pool_onehot(pool, n):
            k, u = n
            pool.wait_ge(s["any_done"], 2 * (k + 1))
            if not (isinstance(k, int) and k <= 1):
                pool.wait_ge(s["st_made"], KT * (k - 1))
            if not (isinstance(k, int) and k <= 1):
                pool.wait_ge(s["blocks_done"], k - 1)
            nc.gpsimd.tensor_tensor(qrs[mr, u, :, :, :].rearrange("r p h q -> r (p h q)"), onehot[mr, :],
                                    any_key[mr, 0:1].to_broadcast([S, PAIRS * QW]),
                                    ALU.mult).then_inc(s["onehot_placed"], 1)

        def pool_query(pool, n):
            k, u = n
            pool.wait_ge(s["onehot_placed"], k + 1)
            pool.wait_ge(s["q_copied"], k + 1)
            for h in range(2):
                def own_columns(c):
                    return parity[:, c:c + 1].unsqueeze(2).to_broadcast([64, PAIRS, S])
                nc.gpsimd.tensor_tensor(q_val[:, :, :], q_rows[:, :, :], own_columns(h), ALU.mult)
                nc.gpsimd.tensor_tensor(q_hi[:, :, :], q_rows[:, :, :], own_columns(2 + h), ALU.mult)\
                    .then_inc(s["q_step"], 1)
                pool.wait_ge(s["q_step"], 4 * k + 2 * h + 1)
                nc.gpsimd.tensor_tensor(qrs[0:64, u, :, h, :], q_val[:, :, :], q_hi[:, :, :],
                                        ALU.subtract).then_inc(s["q_step"], 1)
                pool.wait_ge(s["q_step"], 4 * k + 2 * h + 2)

        def units(eng, unit):
            unit(eng, None, (0, 0), None)
            unit(eng, (0, 0), (1, 1), None)
            with eng.Fori(1, B - 2, 2) as i:
                for v in range(2):
                    k = eng.snap(i + v)
                    unit(eng, (k, (1 + v) % 2), (k + 1, v % 2), (k - 1, v % 2))
            unit(eng, (B - 1, 1), None, (B - 2, 0))

        down_banks = [[ring[:, 0, :], ring[:, 1, :]], [ring[:, 2, :], pv[:, :]]]
        TILES = [range(0, 4), range(4, TT)]

        def sp_expert(sp, e, v):
            if e >= 2:
                sp.wait_ge(s["down_made"], 2 * (e - 1))
            sp.dma_start(up_w[:, v, :], d["up_w"][bass.ds(e, 1), :, :].rearrange("e k i -> k (e i)"))\
                .then_inc(expert_loaded[v], 16)
            sp.dma_start(down_w[:, v, :, :],
                         d["down_w"][bass.ds(e, 1), :, :].rearrange("e (c i) h -> i (e c) h", c=HC))\
                .then_inc(expert_loaded[v], 16)

        def pe_up(pe, e, v):
            pe.wait_ge(expert_loaded[v], 16 * turn(e, v))
            for c in range(HC):
                if not isinstance(e, int) or 4 * e + c >= 2:
                    pe.wait_ge(s["hidden_done"], HC * e + c - 1)
                for h in range(2):
                    mm = nc.tensor.matmul(st[:, c % 2, h, 0:HALF], up_w[:, v, c * P:(c + 1) * P],
                                          xnT[:, h * HALF:(h + 1) * HALF], start=True, stop=True)
                mm.then_inc(s["up_made"], 1)

        def act_gelu(act, e, v):
            for c in range(HC):
                act.wait_ge(s["up_made"], HC * e + c + 1)
                if c == 0 and (not isinstance(e, int) or e >= 2):
                    act.wait_ge(s["down_made"], 2 * (e - 1))
                nc.scalar.activation(hidden[:, v, c, :].rearrange("p (h t) -> p h t", h=2),
                                     st[:, c % 2, :, 0:HALF], ACT.Gelu,
                                     bias=up_bias[:, bass.ds(e * HC + c, 1)]).then_inc(s["hidden_done"], 1)

        def pe_down(pe, e, v):
            pe.wait_ge(s["hidden_done"], HC * (e + 1))
            for h in range(2):
                if not isinstance(e, int) or e >= 2:
                    pe.wait_ge(s["mixed"], 2 * (e - 2) + h + 1)
                for i, t in enumerate(TILES[h]):
                    for c in range(HC):
                        mm = nc.tensor.matmul(down_banks[v][h][:, i * P:(i + 1) * P],
                                              hidden[:, v, c, t * P:(t + 1) * P], down_w[:, v, c, :],
                                              start=(c == 0), stop=(c == HC - 1))
                mm.then_inc(s["down_made"], 1)

        def dve_mix(dve, e, v):
            for h in range(2):
                dve.wait_ge(s["down_made"], 2 * e + h + 1)
                if not isinstance(e, int) or e >= 1:
                    dve.wait_ge(s["mixed"], 2 * (e - 1) + h + 1)
                for i, t in enumerate(TILES[h]):
                    op = nc.vector.scalar_tensor_tensor(out=acc[:, t, :], in0=down_banks[v][h][:, i * P:(i + 1) * P],
                                                        scalar=route[:, bass.ds(e, 1), t:t + 1]
                                                        .rearrange("p e t -> p (e t)"),
                                                        in1=acc[:, t, :], op0=ALU.mult, op1=ALU.add)
                op.then_inc(s["mixed"], 1)

        @block.sync
        def _(sp):
            sp.dma_start(xq[mr, :, :], d["x"].rearrange("b q d -> q b d")).then_inc(s["x_loaded"], 16)
            for i, w in enumerate(("qw", "kw", "vw", "ow")):
                sp.dma_start(w_raw[:, i, :], d[w]).then_inc(s["weights_loaded"], 16)
            sp.dma_start(ident[:, :], d["c_ident"]).then_inc(s["weights_loaded"], 16)
            sp_load_batch(sp, (0, 0))
            sp.dma_start(q_bias[mr, :], d["qb"].unsqueeze(0).to_broadcast([S, D])).then_inc(s["consts_loaded"], 16)
            sp.dma_start(k_bias[:, :], d["kb"].unsqueeze(1)).then_inc(s["consts_loaded"], 16)
            sp.dma_start(v_bias[:, :], d["vb"].unsqueeze(1)).then_inc(s["consts_loaded"], 16)
            sp.dma_start(onehot[mr, :], d["c_onehot"]).then_inc(s["consts_loaded"], 16)
            sp.dma_start(parity[:, :], d["c_parity"]).then_inc(s["consts_loaded"], 16)
            sp.dma_start(pick[:, :, :], d["c_pick"]).then_inc(s["consts_loaded"], 16)
            sp.dma_start(own[:, :, :], d["c_own"]).then_inc(s["consts_loaded"], 16)
            sp_load_batch(sp, (1, 1))
            sp.wait_ge(s["ones_set"], 1)
            sp.dma_start(x_tok[:, :, :], d["x"].rearrange("b q d -> (b q) d").rearrange("(t p) d -> p t d", p=P))\
                .then_inc(s["ffn_consts"], 16)
            sp.dma_start(o_bias[:, :], d["ob"].unsqueeze(0).to_broadcast([P, D])).then_inc(s["ffn_consts"], 16)
            sp.dma_start(gate_w[:, :], d["gate_w"]).then_inc(s["ffn_consts"], 16)
            sp.dma_start(gate_b[:, :], d["gate_b"].unsqueeze(0).to_broadcast([P, E])).then_inc(s["ffn_consts"], 16)
            sp.dma_start(up_b_raw[:, :], d["up_b"].rearrange("e (c i) -> (e c) i", c=HC)).then_inc(s["ffn_consts"], 16)
            sp.dma_start(down_b[:, :], d["down_b"]).then_inc(s["ffn_consts"], 16)
            sp.dma_start(rank[:, :], d["c_rank"]).then_inc(s["ffn_consts"], 16)
            sp.dma_start(gates[:, 0:1], d["gx"].unsqueeze(0).to_broadcast([P, 1])).then_inc(s["ffn_consts"], 16)
            sp.dma_start(gates[:, 1:2], d["gf"].unsqueeze(0).to_broadcast([P, 1])).then_inc(s["ffn_consts"], 16)
            sp_expert(sp, 0, 0)
            sp_expert(sp, 1, 1)

            sp_place(sp, (0, 0))
            sp_place_max(sp, (0, 0))
            sp_place(sp, (1, 1))
            sp_load_batch(sp, (2, 0))
            sp_place_max(sp, (1, 1))
            with sp.Fori(2, B - 3, 2) as i:
                for v in range(2):
                    k = sp.snap(i + v)
                    sp_place(sp, (k, v))
                    sp_load_batch(sp, (k + 1, 1 - v))
                    sp_place_max(sp, (k, v))
            sp_place(sp, (B - 2, 0))
            sp_load_batch(sp, (B - 1, 1))
            sp_place_max(sp, (B - 2, 0))
            sp_place(sp, (B - 1, 1))
            sp_place_max(sp, (B - 1, 1))
            for e in range(2, NE):
                sp_expert(sp, e, e % 2)
            x_out = out.rearrange("b q d -> (b q) d").rearrange("(t p) d -> p t d", p=P)
            for h in range(2):
                sp.wait_ge(s["out_ready"], h + 1)
                t0, t1 = TILES[h][0], TILES[h][-1] + 1
                sp.dma_start(x_out[:, t0:t1, :], acc[:, t0:t1, :]).then_inc(s["out_stored"], 16)
            sp.wait_ge(s["out_stored"], 32)

        NFFN = 9
        NCONST = 7

        @block.scalar
        def _(act):
            act.wait_ge(s["w_turned"], 1)
            nc.scalar.activation(w_t[:, :, :].rearrange("p i d -> p (i d)"), ring[:, 0, :],
                                 ACT.Copy).then_inc(s["w_copied"], 1)
            act.wait_ge(s["stats_done"], 2 * B + 1)
            nc.scalar.activation(rstd[mr, :], rstd[mr, :], ACT.Sqrt).then_inc(s["rstd_var"], 1)
            act.wait_ge(s["ln_turned"], 1)
            nc.scalar.activation(lnT[:, 0:8 * S], ring[:, 1, 0:8 * S], ACT.Copy).then_inc(s["ln_copied"], 1)
            act.wait_ge(s["ln_turned"], 2)
            nc.scalar.activation(lnT[:, 8 * S:16 * S], ring[:, 2, 0:8 * S], ACT.Copy).then_inc(s["ln_copied"], 1)
            act.wait_ge(s["consts_loaded"], 16 * NCONST)
            units(act, act_unit)
            act_slot(act, None, ("A", 0), (B - 1, 1))

            act.wait_ge(s["ffn_consts"], 16 * NFFN)
            nc.scalar.activation(tanh_g[:, :], gates[:, :], ACT.Tanh).then_inc(s["gates_tanh"], 1)
            act.wait_ge(s["ffn_var"], 2 * TT + 1)
            nc.scalar.activation(ln_rstd[:, :], ln_rstd[:, :], ACT.Sqrt).then_inc(s["ffn_ln_done"], 1)
            for h in range(2):
                w = P * len(TILES[h])
                act.wait_ge(s["xn_turned"], h + 1)
                nc.scalar.activation(xnT[:, 4 * P * h:4 * P * h + w], down_banks[1][h][:, 0:w],
                                     ACT.Copy).then_inc(s["xn_copied"], 1)
            act.wait_ge(s["bias_turned"], 1)
            nc.scalar.activation(up_bias[:, :], ring[:, 0, 0:NE * HC], ACT.Copy).then_inc(s["bias_copied"], 1)
            act.wait_ge(s["score_raw"], 1)
            nc.scalar.activation(score[:, :, :], score[:, :, :], ACT.Sigmoid).then_inc(s["score_done"], 1)
            act.wait_ge(s["bias_copied"], 1)
            for e in range(2):
                act_gelu(act, e, e)
            for h in range(2):
                w = P * len(TILES[h])
                act.wait_ge(s["route_turned"], h + 1)
                nc.scalar.activation(routeT[:, 4 * P * h:4 * P * h + w], down_banks[0][h][0:NE, 0:w],
                                     ACT.Copy).then_inc(s["route_copied"], 1)
            act_gelu(act, 2, 0)
            with act.Fori(3, NE - 1, 2) as i:
                for v in range(2):
                    act_gelu(act, act.snap(i + v), (1 + v) % 2)

        @block.tensor
        def _(pe):
            pe.wait_ge(s["weights_loaded"], 80)
            for i in range(4):
                mm = nc.tensor.transpose(ring[:, 0, i * P:(i + 1) * P], w_raw[:, i, :], ident[:, :])
            mm.then_inc(s["w_turned"], 1)
            for g in range(2):
                pe.wait_ge(s["ln_done"], B)
                for i in range(8):
                    b = 8 * g + i
                    mm = nc.tensor.matmul(ring[:, 1 + g, i * S:(i + 1) * S], xq[mr, b, :], ident[mr, mr],
                                          start=True, stop=True)
                mm.then_inc(s["ln_turned"], 1)
            pe.wait_ge(s["w_copied"], 1)
            for g in range(4):
                pe.wait_ge(s["ln_copied"], 1 + g // 2)
                for i in range(4):
                    b = 4 * g + i
                    mm = nc.tensor.matmul(st[MROW:MROW + S, g // 2, g % 2, i * D:(i + 1) * D],
                                          lnT[:, b * S:(b + 1) * S], w_t[:, 0, :], start=True, stop=True)
                mm.then_inc(s["q_made"], 1)
            units(pe, pe_unit)
            pe_attn(pe, (B - 1, 1))

            pe.wait_ge(s["attn_stored"], B)
            for h in range(2):
                for i, t in enumerate(TILES[h]):
                    mm = nc.tensor.matmul(down_banks[0][h][:, i * P:(i + 1) * P], attnT[:, t * P:(t + 1) * P],
                                          w_t[:, 3, :], start=True, stop=True)
                mm.then_inc(s["projected"], 1)
            for h in range(2):
                for i, t in enumerate(TILES[h]):
                    pe.wait_ge(s["ffn_var"], 2 * TT + 2 + t + 1)
                    if h == 1:
                        pe.wait_ge(s["normed_done"], B)
                    mm = nc.tensor.transpose(down_banks[1][h][:, i * P:(i + 1) * P], xn[:, t, :], ident[:, :])
                mm.then_inc(s["xn_turned"], 1)
            pe.wait_ge(s["x1_step"], 2)
            pe.wait_ge(s["ffn_consts"], 16 * NFFN)
            nc.tensor.transpose(ring[:, 0, 0:NE * HC], up_b_raw[:, :], ident[0:NE * HC, 0:NE * HC])\
                .then_inc(s["bias_turned"], 1)
            pe.wait_ge(s["xn_copied"], 2)
            for t in range(TT):
                mm = nc.tensor.matmul(ring[:, 1, t * E:(t + 1) * E], xnT[:, t * P:(t + 1) * P], gate_w[:, :],
                                      start=True, stop=True)
            mm.then_inc(s["gate_made"], 1)
            pe_up(pe, 0, 0)
            pe_up(pe, 1, 1)
            pe.wait_ge(s["route_done"], 1)
            pe.wait_ge(s["bias_copied"], 1)
            for h in range(2):
                for i, t in enumerate(TILES[h]):
                    mm = nc.tensor.transpose(down_banks[0][h][0:NE, i * P:(i + 1) * P], route[:, :, t], ident[:, :])
                mm.then_inc(s["route_turned"], 1)
            for h in range(2):
                pe.wait_ge(s["route_copied"], h + 1)
                for i, t in enumerate(TILES[h]):
                    mm = nc.tensor.matmul(down_banks[1][h][:, i * P:(i + 1) * P], routeT[:, t * P:(t + 1) * P],
                                          down_b[:, :], start=True, stop=True)
                mm.then_inc(s["bias_mixed"], 1)
            pe_down(pe, 0, 0)
            pe_up(pe, 2, 0)
            pe.wait_ge(s["acc_ready"], 2)
            pe_down(pe, 1, 1)
            with pe.Fori(2, NE - 2, 2) as i:
                for v in range(2):
                    e = pe.snap(i + v)
                    pe_up(pe, e + 1, (v + 1) % 2)
                    pe_down(pe, e, v)
            pe_down(pe, NE - 1, 0)

        @block.vector
        def _(dve):
            nc.vector.memset(keys[96:P, :, :, :], 1.0).then_inc(s["ones_set"], 1)
            nc.vector.memset(v_ext[:, :, :, :, DH:VW], 1.0).then_inc(s["dve_step"], 1)
            dve.wait_ge(s["x_loaded"], 16)
            for b in range(B):
                nc.vector.bn_stats(stat[mr, b, :], xq[mr, b, :]).then_inc(s["stats_done"], 1)
            for b in range(B):
                dve.wait_ge(s["stats_done"], B if b == 0 else B + b)
                nc.vector.bn_aggr(mv[mr, b, :], stat[mr, b, :]).then_inc(s["stats_done"], 1)
            dve.wait_ge(s["stats_done"], 2 * B)
            nc.vector.tensor_scalar(rstd[mr, :], mv[mr, :, 1:2].rearrange("p b o -> p (b o)"), EPS, None,
                                    ALU.add).then_inc(s["stats_done"], 1)
            dve.wait_ge(s["rstd_var"], 1)
            nc.vector.reciprocal(rstd[mr, :], rstd[mr, :]).then_inc(s["rstd_done"], 1)
            dve.wait_ge(s["rstd_done"], 1)
            for b in range(B):
                nc.vector.tensor_scalar(xq[mr, b, :], xq[mr, b, :], mv[mr, b, 0:1], rstd[mr, b:b + 1],
                                        ALU.subtract, ALU.mult).then_inc(s["ln_done"], 1)
            dve.wait_ge(s["consts_loaded"], 16 * NCONST)
            for g in range(4):
                dve.wait_ge(s["q_made"], g + 1)
                nc.vector.tensor_tensor(q_all[mr, 4 * g:4 * g + 4, :],
                                        st[mr, g // 2, g % 2, :].rearrange("q (b d) -> q b d", b=4),
                                        q_bias[mr, :].unsqueeze(1).to_broadcast([S, 4, D]), ALU.add)\
                    .then_inc(s["dve_step"], 1)
            dve.wait_ge(s["dve_step"], 5)
            nc.vector.tensor_scalar(q_all[mr, :, :], q_all[mr, :, :], float(DH) ** -0.5, None,
                                    ALU.mult).then_inc(s["q_stored"], 1)
            units(dve, dve_unit)
            dve_norm(dve, (B - 1, 1))

            dve.wait_ge(s["gates_tanh"], 1)
            for h in range(2):
                t0, t1 = TILES[h][0], TILES[h][-1] + 1
                dve.wait_ge(s["projected"], h + 1)
                nc.vector.tensor_tensor(xn[:, t0:t1, :],
                                        down_banks[0][h][:, 0:(t1 - t0) * P].rearrange("p (t d) -> p t d", d=D),
                                        o_bias[:, :].unsqueeze(1).to_broadcast([P, t1 - t0, D]),
                                        ALU.add).then_inc(s["x1_step"], 1)
            for h in range(2):
                t0, t1 = TILES[h][0], TILES[h][-1] + 1
                dve.wait_ge(s["x1_step"], h + 1)
                nc.vector.scalar_tensor_tensor(out=x_tok[:, t0:t1, :], in0=xn[:, t0:t1, :], scalar=tanh_g[:, 0:1],
                                               in1=x_tok[:, t0:t1, :], op0=ALU.mult,
                                               op1=ALU.add).then_inc(s["x1_done"], 1)
            for t in range(TT):
                if t in (0, 4):
                    dve.wait_ge(s["x1_done"], 1 + t // 4)
                nc.vector.bn_stats(ln_stat[:, t, :], x_tok[:, t, :]).then_inc(s["ffn_var"], 1)
            dve.wait_ge(s["ffn_var"], TT)
            for t in range(TT):
                nc.vector.bn_aggr(ln_mv[:, t, :], ln_stat[:, t, :]).then_inc(s["ffn_var"], 1)
            dve.wait_ge(s["ffn_var"], 2 * TT)
            nc.vector.tensor_scalar(ln_rstd[:, :], ln_mv[:, :, 1:2].rearrange("p t o -> p (t o)"), EPS, None,
                                    ALU.add).then_inc(s["ffn_var"], 1)
            dve.wait_ge(s["ffn_ln_done"], 1)
            nc.vector.reciprocal(ln_rstd[:, :], ln_rstd[:, :]).then_inc(s["ffn_var"], 1)
            dve.wait_ge(s["ffn_var"], 2 * TT + 2)
            for t in range(TT):
                nc.vector.tensor_scalar(xn[:, t, :], x_tok[:, t, :], ln_mv[:, t, 0:1], ln_rstd[:, t:t + 1],
                                        ALU.subtract, ALU.mult).then_inc(s["ffn_var"], 1)

            dve.wait_ge(s["gate_made"], 1)
            nc.vector.tensor_tensor(score[:, :, :], ring[:, 1, 0:TT * E].rearrange("p (t e) -> p t e", e=E),
                                    gate_b[:, :].unsqueeze(1).to_broadcast([P, TT, E]),
                                    ALU.add).then_inc(s["score_raw"], 1)
            dve.wait_ge(s["score_done"], 1)
            steps = [0]

            def then(op):
                op.then_inc(s["route_step"], 1)
                steps[0] += 1
                dve.wait_ge(s["route_step"], steps[0])

            def over_experts(v):
                return v.unsqueeze(2).to_broadcast([P, TT, E])

            rank3 = rank[:, :].rearrange("p (t e) -> p t e", e=E)
            then(nc.vector.memset(route[:, E, :], 1.0))
            for r, chosen in enumerate((pick1, pick2)):
                then(nc.vector.tensor_reduce(topv[:, r, :], score[:, :, :], AX.X, ALU.max))
                then(nc.vector.tensor_tensor(tmp[:, :, :], score[:, :, :], over_experts(topv[:, r, :]), ALU.is_equal))
                then(nc.vector.tensor_tensor(tmp[:, :, :], tmp[:, :, :], rank3, ALU.mult))
                then(nc.vector.tensor_reduce(tmpv[:, :], tmp[:, :, :], AX.X, ALU.max))
                then(nc.vector.tensor_tensor(chosen[:, :, :], tmp[:, :, :], over_experts(tmpv[:, :]), ALU.is_equal))
                if r == 0:
                    then(nc.vector.scalar_tensor_tensor(out=score[:, :, :], in0=chosen[:, :, :], scalar=-4.0,
                                                        in1=score[:, :, :], op0=ALU.mult, op1=ALU.add))
            then(nc.vector.scalar_tensor_tensor(out=tmpv[:, :], in0=topv[:, 0, :], scalar=1e-6, in1=topv[:, 1, :],
                                                op0=ALU.add, op1=ALU.add))
            then(nc.vector.reciprocal(tmpv[:, :], tmpv[:, :]))
            for r, chosen in enumerate((pick1, pick2)):
                then(nc.vector.tensor_tensor(topv[:, r, :], topv[:, r, :], tmpv[:, :], ALU.mult))
                then(nc.vector.tensor_tensor(chosen[:, :, :], chosen[:, :, :], over_experts(topv[:, r, :]), ALU.mult))
            nc.vector.tensor_tensor(route[:, 0:E, :].rearrange("p e t -> p t e"), pick1[:, :, :], pick2[:, :, :],
                                    ALU.add).then_inc(s["route_done"], 1)
            for h in range(2):
                t0, t1 = TILES[h][0], TILES[h][-1] + 1
                dve.wait_ge(s["bias_mixed"], h + 1)
                nc.vector.tensor_copy(acc[:, t0:t1, :].rearrange("p t d -> p (t d)"),
                                      down_banks[1][h][:, 0:(t1 - t0) * P]).then_inc(s["acc_ready"], 1)
            dve.wait_ge(s["acc_ready"], 2)
            dve.wait_ge(s["route_done"], 1)
            dve_mix(dve, 0, 0)
            dve_mix(dve, 1, 1)
            with dve.Fori(2, NE - 2, 2) as i:
                for v in range(2):
                    dve_mix(dve, dve.snap(i + v), v)
            dve_mix(dve, NE - 1, 0)
            dve.wait_ge(s["mixed"], 2 * NE)
            nc.vector.tensor_reduce(tmpv[:, :], acc[:, :, :], AX.X, ALU.max,
                                    apply_absolute_value=True).then_inc(s["out_step"], 1)
            dve.wait_ge(s["out_step"], 1)
            nc.vector.tensor_scalar(tmpv[:, :], tmpv[:, :], 0.1, 1e-6, ALU.mult, ALU.add).then_inc(s["out_step"], 1)
            dve.wait_ge(s["out_step"], 2)
            nc.vector.reciprocal(tmpv[:, :], tmpv[:, :]).then_inc(s["out_step"], 1)
            dve.wait_ge(s["out_step"], 3)
            nc.vector.tensor_scalar(tmpv[:, :], tmpv[:, :], tanh_g[:, 1:2], 0.1, ALU.mult,
                                    ALU.mult).then_inc(s["out_step"], 1)
            dve.wait_ge(s["out_step"], 4)
            for h in range(2):
                for t in TILES[h]:
                    op = nc.vector.scalar_tensor_tensor(out=acc[:, t, :], in0=acc[:, t, :], scalar=tmpv[:, t:t + 1],
                                                        in1=x_tok[:, t, :], op0=ALU.mult, op1=ALU.add)
                op.then_inc(s["out_ready"], 1)

        @block.gpsimd
        def _(pool):
            nc.gpsimd.memset(blocks[:, :, :], 0.0).then_inc(s["blocks_zeroed"], 1)
            pool.wait_ge(s["blocks_zeroed"], 1)
            pool.wait_ge(s["consts_loaded"], 16 * NCONST)
            pool.wait_ge(s["q_stored"], 1)
            units(pool, pool_unit)
            pool_blocks(pool, (B - 1, 1))


_INS = {
    "x": "x", "ctx": "ctx_1024", "mask": "mask_BxSxS2_if1", "gx": "g_xattn", "gf": "g_ffn",
    "qw": "L0_xattn_qw", "qb": "L0_xattn_qb", "kw": "L0_xattn_kw", "kb": "L0_xattn_kb",
    "vw": "L0_xattn_vw", "vb": "L0_xattn_vb", "ow": "L0_xattn_ow", "ob": "L0_xattn_ob",
    "gate_w": "L0_ffn_gate_w", "gate_b": "L0_ffn_bias",
}


def kernel(**inputs):
    import concourse.bacc as _bacc
    from concourse.bass_utils import run_bass_kernel_spmd as _run

    arrays = {k: np.ascontiguousarray(inputs[v]) for k, v in _INS.items()}
    for k, routed, shared in (("up_w", "L0_ffn_up_w", "L0_ffn_sw_up"), ("up_b", "L0_ffn_up_b", "L0_ffn_sb_up"),
                              ("down_w", "L0_ffn_down_w", "L0_ffn_sw_down"),
                              ("down_b", "L0_ffn_down_b", "L0_ffn_sb_down")):
        arrays[k] = np.concatenate([np.asarray(inputs[routed]), np.asarray(inputs[shared])[None]])
    arrays.update(constants())
    nc = _bacc.Bacc("TRN2", target_bir_lowering=False, num_devices=1)
    feeds, aps = {}, {}
    for k, a in arrays.items():
        feeds["in_" + k] = a
        aps[k] = nc.dram_tensor("in_" + k, a.shape, mybir.dt.from_np(a.dtype), kind="ExternalInput").ap()
    out = nc.dram_tensor("out_0", (B, S, D), F32, kind="ExternalOutput").ap()
    flamingo_kernel(nc, aps, out)
    r = _run(nc, [feeds], core_ids=[0])
    return r.results[0]["out_0"]
```

```python
from contextlib import ExitStack

import numpy as np
import concourse.bass as bass
from concourse import mybir

ALU = mybir.AluOpType
ACT = mybir.ActivationFunctionType
F32 = mybir.dt.float32
F16 = mybir.dt.float16
I32 = mybir.dt.int32
AX = mybir.AxisListType

P = 128
B, S, D, H = 16, 56, 128, 16
DH = D // H
NK = 1500
KT = 12
KLAST = NK - (KT - 1) * P
PAIRS = H // 2
QW = 2 * S
HQ = H * S
RT = HQ // P
TOK = B * S
TT = TOK // P
MROW = 64
ONEROW = 96
QSPLIT = ONEROW - MROW
NR = S + 1
ROWS = MROW + NR
NCH = 3
CH = 512
VW = DH + 1
WIN = 4
H0 = [min(P * t // S, H - WIN) for t in range(RT)]
BIG = 32768.0
E = 8
NE = E + 1
HID = 4 * D
HC = HID // P
EPS = 1e-5
HALF = TOK // 2


def constants():
    row = np.arange(HQ).reshape(RT, P)
    head, query = row // S, row % S
    pick = (query[:, :, None] == np.arange(S)).transpose(1, 0, 2).astype(np.float32)
    own = (head[:, :, None] == (np.array(H0)[:, None] + np.arange(WIN))[:, None, :])
    own = np.repeat(own.transpose(1, 0, 2)[..., None], DH, axis=3).reshape(P, RT, WIN * DH)
    skip = np.insert(np.eye(S, dtype=np.float32), QSPLIT, 0.0, axis=0)
    onehot = np.tile(skip.astype(np.float16) * np.float16(BIG), (1, 2 * PAIRS))
    parity = ((np.arange(4 * 2 * DH) // DH % 2)[:, None] == np.arange(2)).astype(np.float32)
    parity = np.concatenate([parity, parity * (np.arange(64) >= 32)[:, None]], axis=1).astype(np.float32)
    rank = np.tile(np.arange(E, 0, -1, dtype=np.float32), (P, TT))
    return {
        "c_ident": np.eye(P, dtype=np.float32),
        "c_pick": pick,
        "c_own": own.astype(np.float32),
        "c_skip": skip,
        "c_onehot": onehot,
        "c_parity": parity,
        "c_rank": rank,
    }


def flamingo_kernel(nc, d, out):
    with ExitStack() as ctx:
        def sb(name, shape, dt=F32):
            return ctx.enter_context(nc.sbuf_tensor(name, shape, dt))

        def sem(name):
            return ctx.enter_context(nc.semaphore(name))

        ident = sb("ident", [P, P])
        pick = sb("pick", [P, RT, S])
        skip = sb("skip", [P, S])
        own = sb("own", [P, RT, WIN * DH])
        onehot = sb("onehot", [P, PAIRS * QW], F16)
        parity = sb("parity", [64, 4])
        rank = sb("rank", [P, TT * E])
        w_raw = sb("w_raw", [P, 4, D])
        w_t = sb("w_t", [P, 4, D])
        q_bias = sb("q_bias", [P, D])
        k_bias = sb("k_bias", [P, 1])
        v_bias = sb("v_bias", [P, 1])
        gates = sb("gates", [P, 2])
        tanh_g = sb("tanh_g", [P, 2])
        xq = sb("xq", [P, B, D])
        stat = sb("stat", [P, B, 6])
        mv = sb("mv", [P, B, 2])
        rstd = sb("rstd", [P, B])
        lnT = sb("lnT", [P, B * NR])
        q_all = sb("q_all", [P, B, D])
        q_any = sb("q_any", [P, PAIRS, 4, 16])
        q_rows = sb("q_rows", [64, PAIRS, S])
        q_val = sb("q_val", [64, PAIRS, S])
        q_hi = sb("q_hi", [64, PAIRS, S], F16)
        mask_raw = sb("mask_raw", [P, 2, NK], I32)
        mask_abs = sb("mask_abs", [P, 1])
        any_key = sb("any_key", [P, 1])
        fill = sb("fill", [P, 1])
        mask_add = sb("mask_add", [P, NK], F16)
        ctx_raw = sb("ctx_raw", [P, 2, KT, D])
        ctxT = sb("ctxT", [P, NK])
        k_hi = sb("k_hi", [P, NK], F16)
        k_lo = sb("k_lo", [P, NK], F16)
        keys = sb("keys", [P, 2, PAIRS, NK], F16)
        qrs = sb("qrs", [P, 2, PAIRS, 2, S], F16)
        q_stage = sb("q_stage", [P, PAIRS, 2, S], F16)
        v_ext = sb("v_ext", [P, 2, KT, H, VW])
        max_part = sb("max_part", [QW, PAIRS, NCH])
        neg_max = sb("neg_max", [QW, PAIRS])
        probs = sb("probs", [P, 3, HQ])
        recip = sb("recip", [P, RT])
        normed = sb("normed", [P, RT, WIN * DH])
        blocks = sb("blocks", [P, RT, D])
        attnT = sb("attnT", [P, TOK])

        x_tok = sb("x_tok", [P, TT, D])
        o_bias = sb("o_bias", [P, D])
        gate_w = sb("gate_w", [P, E])
        gate_b = sb("gate_b", [P, E])
        up_b_raw = sb("up_b_raw", [NE * HC, P])
        up_bias = sb("up_bias", [P, NE * HC])
        down_b = sb("down_b", [NE, D])
        up_w = sb("up_w", [P, 2, HID])
        down_w = sb("down_w", [P, 2, HC, D])
        ln_stat = sb("ln_stat", [P, TT, 6])
        ln_mv = sb("ln_mv", [P, TT, 2])
        ln_rstd = sb("ln_rstd", [P, TT])
        xn = sb("xn", [P, TT, D])
        xnT = lnT[:, 0:TOK]
        score = sb("score", [P, TT, E])
        topv = sb("topv", [P, 2, TT])
        pick1 = sb("pick1", [P, TT, E])
        pick2 = sb("pick2", [P, TT, E])
        tmp = sb("tmp", [P, TT, E])
        tmpv = sb("tmpv", [P, TT])
        route = sb("route", [P, NE, TT])
        routeT = sb("routeT", [NE, TOK])
        acc = sb("acc", [P, TT, D])
        hidden = keys[:, :, :, :].rearrange("p u a k -> p (u a k)").bitcast(F32)[:, 0:2 * HC * TOK]\
            .rearrange("p (u c t) -> p u c t", u=2, c=HC)

        k_dram = nc.dram_tensor("k_dram", (2, P, NK), F16, kind="Internal").ap()
        ring = ctx.enter_context(nc.psum_tensor("ring", [P, 3, 512], F32))
        st = ctx.enter_context(nc.psum_tensor("st", [P, 2, 2, 512], F32))
        pv = ctx.enter_context(nc.psum_tensor("pv", [P, 512], F32))
        pv_win = pv[:, 0:RT * WIN * VW].rearrange("p (t h w) -> p t h w", t=RT, h=WIN)

        names = """
        consts_loaded weights_loaded x_loaded k_spilled ones_set
        w_turned w_copied stats_done rstd_var rstd_done ln_done ln_turned ln_copied q_made q_stored
        ctx_turned ctx_copied k_made k_hi_stored k_lo_stored v_made v_stored
        mask_abs_done any_done mask_ready onehot_placed q_blanked q_spread q_copied q_step blocks_zeroed
        q_moved scored max_read max_merged max_turned max_copied
        st_made exps_done pv_done recip_done normed_done blocks_done attn_made attn_stored dve_step
        ffn_consts gates_tanh projected x1_step x1_done ffn_var ffn_ln_done xn_turned xn_copied bias_turned
        bias_copied gate_made score_raw score_done route_step route_done route_turned route_copied
        bias_mixed acc_ready up_made hidden_done down_made mixed out_step out_ready out_stored
        """.split()
        s = {n: sem("s_" + n) for n in names}
        ctx_loaded = [sem(f"s_ctx_loaded{u}") for u in range(2)]
        mask_loaded = [sem(f"s_mask_loaded{u}") for u in range(2)]
        up_loaded = [sem(f"s_up_loaded{u}") for u in range(2)]
        down_loaded = [sem(f"s_down_loaded{u}") for u in range(2)]

        def turn(k, u):
            return k - u + 2

        keys_placed = [sem(f"s_keys_placed{c}") for c in range(NCH)]

        block = ctx.enter_context(nc.Block())

        mr = slice(MROW, ROWS)
        QA, QB = slice(MROW, ONEROW), slice(ONEROW + 1, ROWS)


        def known(k, below):
            return isinstance(k, int) and k < below

        def tile_keys(j):
            return P if j < KT - 1 else KLAST

        def chunk(c):
            return slice(c * CH, min((c + 1) * CH, NK))

        S_PER_STEP = [0, 2, 2, 3, 3, 3, 3, 3, 3, 2, 0, 0]
        STEPS, done = [], 0
        for j, count in enumerate(S_PER_STEP):
            STEPS.append({0: [("V", 0), ("V", 1), ("V", 2)], 1: [("T", 0), ("T", 1), ("T", 2)],
                          2: [("K", 0), ("K", 1), ("K", 2)], 3: [("A", 0)],
                          KT - 1: [("M", 0), ("M", 1), None, None]}.get(j, [])
                         + [("S", done + i) for i in range(count)])
            done += count
        STEPS[4].insert(1, ("Q", 0))
        ORDER = [slot for step in STEPS for slot in step]
        assert done == PAIRS * NCH and len(ORDER) % 3 == 0
        RING = {slot: i % 3 for i, slot in enumerate(ORDER) if slot}
        KIND = {"V": (1, NCH, "v_stored"), "T": (2, NCH, "ctx_copied"), "K": (2, NCH, "k_lo_stored"),
                "Q": (2, 1, "q_copied"), "A": (-1, 1, "attn_stored"), "S": (1, PAIRS * NCH, "max_read"),
                "M": (1, 2, "max_copied")}

        def present(slot, k):
            off = KIND[slot[0]][0]
            return not isinstance(k, int) or 0 <= k + off < B

        def ring_free(pe, k, slot):
            i = ORDER.index(slot)
            while True:
                i -= 3
                if i < 0:
                    i, k = i + len(ORDER), k - 1
                if known(k, -2):
                    return
                if ORDER[i] and present(ORDER[i], k):
                    off, count, name = KIND[ORDER[i][0]]
                    pe.wait_ge(s[name], count * (k + off) + ORDER[i][1] + 1)
                    return

        def sp_load_batch(sp, n):
            k, u = n
            src = d["ctx"][bass.ds(k, 1), :, :]
            sp.dma_start(ctx_raw[:, u, 0:KT - 1, :],
                         src[:, 0:(KT - 1) * P, :].rearrange("b (t p) d -> p (b t) d", p=P)).then_inc(ctx_loaded[u], 16)
            sp.dma_start(ctx_raw[0:KLAST, u, KT - 1, :],
                         src[:, (KT - 1) * P:NK, :].rearrange("b p d -> p (b d)")).then_inc(ctx_loaded[u], 16)
            msk = d["mask"][bass.ds(k, 1), :, :].rearrange("b q k -> q (b k)")
            sp.dma_start(mask_raw[QA, u, :], msk[0:QSPLIT, :]).then_inc(mask_loaded[u], 16)
            sp.dma_start(mask_raw[QB, u, :], msk[QSPLIT:S, :]).then_inc(mask_loaded[u], 16)

        def sp_place(sp, n, c):
            k, u = n
            if not known(k, 2):
                sp.wait_ge(s["st_made"], KT * (k - 2) + 4 * (c + 1))
            for rows in (QA, QB):
                nq = rows.stop - rows.start
                sp.dma_start(keys[rows, u, :, chunk(c)],
                             mask_add[rows, chunk(c)].unsqueeze(1).to_broadcast([nq, PAIRS, chunk(c).stop - c * CH]))\
                    .then_inc(keys_placed[c], 16)
            if c == 0:
                sp.wait_ge(s["k_spilled"], 32 * (k + 1))
            for r in range(4):
                sp.dma_start(keys[16 * r:16 * r + 16, u, :, chunk(c)],
                             k_dram[r % 2, :, chunk(c)].rearrange("(p i) k -> i p k", i=16))\
                    .then_inc(keys_placed[c], 16)

        def sp_unit(sp, b):
            k, u = b
            n = (k + 2, u)
            if not known(k, -2) and not (isinstance(k, int) and k + 2 >= B):
                sp.wait_ge(s["k_lo_stored"], NCH * (k + 3))
                sp.dma_start(k_dram[0], k_hi[:, :]).then_inc(s["k_spilled"], 16)
                sp.dma_start(k_dram[1], k_lo[:, :]).then_inc(s["k_spilled"], 16)
                if not (isinstance(k, int) and (k + 3 >= B or k + 3 < 2)):
                    sp_load_batch(sp, (k + 3, 1 - u))
                for c in range(NCH):
                    sp_place(sp, n, c)

        def pe_ctx_turn(pe, b, c):
            k, u = b
            ring_free(pe, k, ("T", c))
            if c == 0:
                pe.wait_ge(ctx_loaded[u], 16 * turn(k + 2, u))
            for i in range(4):
                j = 4 * c + i
                m = tile_keys(j)
                mm = nc.tensor.transpose(ring[:, RING[("T", c)], i * P:i * P + m],
                                         ctx_raw[0:m, u, j, :], ident[0:m, 0:m])
            mm.then_inc(s["ctx_turned"], 1)

        def pe_k(pe, b, c):
            k, u = b
            ring_free(pe, k, ("K", c))
            pe.wait_ge(s["ctx_copied"], NCH * (k + 2) + c + 1)
            w = chunk(c).stop - c * CH
            nc.tensor.matmul(ring[:, RING[("K", c)], 0:w], w_t[:, 1, :], ctxT[:, chunk(c)],
                             start=True, stop=True).then_inc(s["k_made"], 1)

        def pe_v(pe, b, c):
            k, u = b
            ring_free(pe, k, ("V", c))
            for i in range(4):
                j = 4 * c + i
                m = tile_keys(j)
                mm = nc.tensor.matmul(ring[0:m, RING[("V", c)], i * P:(i + 1) * P], ctxT[:, j * P:j * P + m],
                                      w_t[:, 2, :], start=True, stop=True)
            mm.then_inc(s["v_made"], 1)

        def pe_q_waits(pe, b):
            ring_free(pe, b[0], ("Q", 0))
            pe.wait_ge(s["q_blanked"], b[0] + 3)

        def pe_q(pe, b):
            bank = ring[0:64, RING[("Q", 0)], 0:PAIRS * S].rearrange("r (p q) -> r p q", p=PAIRS)
            for p in range(PAIRS):
                mm = nc.tensor.matmul(bank[:, p, :], q_any[mr, p, :, :].rearrange("q r d -> q (r d)"),
                                      skip[mr, :], start=True, stop=True)
            mm.then_inc(s["q_spread"], 1)

        def pe_score(pe, b, m):
            k, u = b
            c, p = divmod(m, PAIRS)
            w = chunk(c).stop - c * CH
            ring_free(pe, k, ("S", m))
            if m == 0:
                pe.wait_ge(s["q_moved"], k + 2)
            if p == 0:
                pe.wait_ge(keys_placed[c], 96 * (k + 2))
            nc.tensor.matmul(ring[0:QW, RING[("S", m)], 0:w],
                             qrs[0:ROWS, 1 - u, p, :, :].rearrange("r h q -> r (h q)"),
                             keys[0:ROWS, 1 - u, p, chunk(c)], start=True, stop=True).then_inc(s["scored"], 1)

        def pe_max_row(pe, b, g):
            k, u = b
            ring_free(pe, k, ("M", g))
            if g == 0:
                pe.wait_ge(s["max_merged"], k + 2)
            for i in range(4):
                mm = nc.tensor.matmul(ring[ONEROW:ONEROW + 1, RING[("M", g)], i * QW:(i + 1) * QW],
                                      neg_max[:, 4 * g + i:4 * g + i + 1], ident[0:QW, 0:QW], start=True, stop=True)
            mm.then_inc(s["max_turned"], 1)

        def pe_scores_t(pe, b, j):
            k, u = b
            m = tile_keys(j)
            if j == 0:
                pe.wait_ge(s["max_copied"], 2 * (k + 1))
            if j >= 2 or not known(k, 1):
                pe.wait_ge(s["exps_done"], KT * k + j - 1)
            for p in range(PAIRS):
                mm = nc.tensor.matmul(st[0:m, j % 2, p // 4, QW * (p % 4):QW * (p % 4 + 1)],
                                      keys[0:ROWS, u, p, j * P:j * P + m],
                                      qrs[0:ROWS, u, p, :, :].rearrange("r h q -> r (h q)"),
                                      start=True, stop=True)
            mm.then_inc(s["st_made"], 1)

        def pe_pv(pe, b, j):
            k, u = b
            m = tile_keys(j)
            pe.wait_ge(s["exps_done"], KT * k + j + 1)
            if j == 0:
                pe.wait_ge(s["v_stored"], NCH * (k + 1))
                if not known(k, 1):
                    pe.wait_ge(s["normed_done"], k)
            for t in range(RT):
                mm = nc.tensor.matmul(pv_win[:, t, :, :].rearrange("p h w -> p (h w)"),
                                      probs[0:m, j % 3, t * P:(t + 1) * P],
                                      v_ext[0:m, u, j, H0[t]:H0[t] + WIN, :].rearrange("p h w -> p (h w)"),
                                      start=(j == 0 and t == 0), stop=(j == KT - 1), skip_group_check=True)
            mm.then_inc(s["pv_done"], 1)

        def pe_attn(pe, b):
            k, u = b
            if known(-k if isinstance(k, int) else k, -B + 1):
                pe.wait_ge(s["attn_stored"], B - 1)
            else:
                ring_free(pe, k, ("A", 0))
            pe.wait_ge(s["blocks_done"], k)
            for t in range(RT):
                mm = nc.tensor.matmul(ring[:, RING[("A", 0)], 0:S], blocks[:, t, :], pick[:, t, :],
                                      start=(t == 0), stop=(t == RT - 1))
            mm.then_inc(s["attn_made"], 1)

        PE_SLOT = {"T": pe_ctx_turn, "K": pe_k, "V": pe_v, "S": pe_score, "M": pe_max_row,
                   "Q": lambda pe, b, c: pe_q(pe, b), "A": lambda pe, b, c: pe_attn(pe, b)}

        def attends(k):
            return not isinstance(k, int) or k >= 0

        def pe_unit(pe, b):
            k, u = b
            for j in range(KT):
                if j == 4 and present(("Q", 0), k):
                    pe_q_waits(pe, b)
                for slot in STEPS[j]:
                    if slot and slot[0] != "M" and present(slot, k):
                        PE_SLOT[slot[0]](pe, b, slot[1])
                if attends(k):
                    pe_scores_t(pe, b, j)
                    if j > 0:
                        pe_pv(pe, b, j - 1)
            for g in range(2):
                if present(("M", g), k):
                    pe_max_row(pe, b, g)
            if attends(k):
                pe_pv(pe, b, KT - 1)

        def act_ctx(act, b, c):
            k, u = b
            act.wait_ge(s["ctx_turned"], NCH * (k + 2) + c + 1)
            if c == 0 and not known(k, -1):
                act.wait_ge(s["v_made"], NCH * (k + 2))
            w = chunk(c).stop - c * CH
            nc.scalar.activation(ctxT[:, chunk(c)], ring[:, RING[("T", c)], 0:w],
                                 ACT.Copy).then_inc(s["ctx_copied"], 1)

        def act_k_hi(act, b, c):
            k, u = b
            act.wait_ge(s["k_made"], NCH * (k + 2) + c + 1)
            if c == 0 and not known(k, -1):
                for x in keys_placed:
                    act.wait_ge(x, 96 * (k + 2))
            w = chunk(c).stop - c * CH
            nc.scalar.activation(k_hi[:, chunk(c)], ring[:, RING[("K", c)], 0:w], ACT.Identity,
                                 bias=k_bias[:, 0:1]).then_inc(s["k_hi_stored"], 1)

        def act_v(act, b, c):
            k, u = b
            act.wait_ge(s["v_made"], NCH * (k + 1) + c + 1)
            if c == 0 and not known(k, 1):
                act.wait_ge(s["pv_done"], KT * k)
            full = 4 if c < NCH - 1 else 3
            src = ring[:, RING[("V", c)], :].rearrange("p (i h w) -> p i h w", i=4, h=H)
            if c == NCH - 1:
                nc.scalar.activation(v_ext[0:KLAST, 1 - u, KT - 1, :, 0:DH], src[0:KLAST, 3], ACT.Copy)
            nc.scalar.activation(v_ext[:, 1 - u, 4 * c:4 * c + full, :, 0:DH], src[:, 0:full],
                                 ACT.Copy).then_inc(s["v_stored"], 1)

        def act_query(act, b):
            k, u = b
            act.wait_ge(s["any_done"], 2 * (k + 3))
            if not known(k, -1):
                act.wait_ge(s["q_spread"], k + 2)
            nc.scalar.activation(q_any[mr, :, :, :],
                                 q_all[mr, bass.ds(k + 2, 1), :].rearrange("q b (p d) -> q (b p) d", p=PAIRS)
                                 .unsqueeze(2).to_broadcast([NR, PAIRS, 4, 16]),
                                 ACT.Copy, scale=any_key[mr, 0:1]).then_inc(s["q_blanked"], 1)

        def act_q_rows(act, b):
            k, u = b
            act.wait_ge(s["q_spread"], k + 3)
            if not known(k, -1):
                act.wait_ge(s["q_step"], 4 * (k + 2))
            nc.scalar.activation(q_rows[:, :, :].rearrange("r p q -> r (p q)"),
                                 ring[0:64, RING[("Q", 0)], 0:PAIRS * S], ACT.Copy).then_inc(s["q_copied"], 1)

        def act_attn(act, b):
            k, u = b
            act.wait_ge(s["attn_made"], k)
            nc.scalar.activation(attnT[:, bass.ds((k - 1) * S, S)], ring[:, RING[("A", 0)], 0:S], ACT.Identity,
                                 bias=v_bias[:, 0:1]).then_inc(s["attn_stored"], 1)

        def act_max_row(act, b, g):
            k, u = b
            act.wait_ge(s["max_turned"], 2 * (k + 1) + g + 1)
            nc.scalar.activation(qrs[ONEROW:ONEROW + 1, 1 - u, 4 * g:4 * g + 4, :, :].rearrange("r p h q -> r (p h q)"),
                                 ring[ONEROW:ONEROW + 1, RING[("M", g)], 0:4 * QW],
                                 ACT.Copy).then_inc(s["max_copied"], 1)

        def act_exp(act, b, j):
            k, u = b
            m = tile_keys(j)
            act.wait_ge(s["st_made"], KT * k + j + 1)
            if j >= 3 or not known(k, 1):
                act.wait_ge(s["pv_done"], KT * k + j - 2)
            nc.scalar.activation(probs[0:m, j % 3, :].rearrange("p (h c) -> p h c", h=2),
                                 st[0:m, j % 2, :, 0:HQ // 2], ACT.Exp).then_inc(s["exps_done"], 1)

        ACT_SLOT = {"T": act_ctx, "K": act_k_hi, "V": act_v,
                    "Q": lambda act, b, c: act_q_rows(act, b), "A": lambda act, b, c: act_attn(act, b)}

        def act_unit(act, b):
            k, u = b
            for j in range(KT):
                if j == 3 and present(("Q", 0), k):
                    act_query(act, b)
                for slot in STEPS[j]:
                    if slot and slot[0] in ACT_SLOT and present(slot, k):
                        ACT_SLOT[slot[0]](act, b, slot[1])
                if attends(k):
                    act_exp(act, b, j)
            for g in range(2):
                if present(("M", g), k):
                    act_max_row(act, b, g)

        def dve_mask(dve, b):
            k, u = b
            dve.wait_ge(mask_loaded[u], 16 * turn(k + 2, u))
            nc.vector.tensor_reduce(mask_abs[mr, :], mask_raw[mr, u, :], AX.X, ALU.max,
                                    apply_absolute_value=True).then_inc(s["mask_abs_done"], 1)
            dve.wait_ge(s["mask_abs_done"], k + 3)
            if not known(k, -1):
                dve.wait_ge(s["q_blanked"], k + 2)
                dve.wait_ge(s["onehot_placed"], k + 2)
            nc.vector.tensor_scalar(any_key[mr, :], mask_abs[mr, :], 0.0, None,
                                    ALU.is_gt).then_inc(s["any_done"], 1)
            dve.wait_ge(s["any_done"], 2 * (k + 2) + 1)
            nc.vector.tensor_scalar(fill[mr, :], any_key[mr, :], -BIG, None, ALU.mult).then_inc(s["any_done"], 1)
            dve.wait_ge(s["any_done"], 2 * (k + 2) + 2)
            if not known(k, -1):
                for x in keys_placed:
                    dve.wait_ge(x, 96 * (k + 2))
            nc.vector.tensor_scalar(mask_add[mr, :], mask_raw[mr, u, :], 0.0, fill[mr, 0:1],
                                    ALU.is_equal, ALU.mult).then_inc(s["mask_ready"], 1)

        def dve_k_lo(dve, b, c):
            k, u = b
            dve.wait_ge(s["k_hi_stored"], NCH * (k + 2) + c + 1)
            w = chunk(c).stop - c * CH
            nc.vector.scalar_tensor_tensor(out=k_lo[:, chunk(c)], in0=ring[:, RING[("K", c)], 0:w],
                                           scalar=k_bias[:, 0:1], in1=k_hi[:, chunk(c)],
                                           op0=ALU.add, op1=ALU.subtract).then_inc(s["k_lo_stored"], 1)

        def dve_move_q(dve, b):
            k, u = b
            dve.wait_ge(s["q_step"], 4 * (k + 2))
            if not known(k, 1):
                dve.wait_ge(s["st_made"], KT * k)
            nc.vector.tensor_copy(qrs[0:ROWS, 1 - u, :, :, :].rearrange("r p h q -> r (p h q)"),
                                  q_stage[0:ROWS, :, :, :].rearrange("r p h q -> r (p h q)"))\
                .then_inc(s["q_moved"], 1)

        def dve_max(dve, b, m):
            k, u = b
            c, p = divmod(m, PAIRS)
            w = chunk(c).stop - c * CH
            dve.wait_ge(s["scored"], PAIRS * NCH * (k + 1) + m + 1)
            nc.vector.tensor_reduce(max_part[:, p, c:c + 1], ring[0:QW, RING[("S", m)], 0:w], AX.X,
                                    ALU.max).then_inc(s["max_read"], 1)

        def dve_merge_max(dve, b):
            k, u = b
            dve.wait_ge(s["max_read"], PAIRS * NCH * (k + 2))
            if not known(k, 0):
                dve.wait_ge(s["max_turned"], 2 * (k + 1))
            nc.vector.tensor_reduce(neg_max[:, :], max_part[:, :, :], AX.X, ALU.max,
                                    negate=True).then_inc(s["max_merged"], 1)

        def dve_norm(dve, b):
            k, u = b
            dve.wait_ge(s["pv_done"], KT * k)
            nc.vector.reciprocal(recip[:, :], pv_win[:, :, WIN - 1, DH:VW]).then_inc(s["recip_done"], 1)
            dve.wait_ge(s["recip_done"], k)
            if not known(k, 2):
                dve.wait_ge(s["blocks_done"], k - 1)
            nc.vector.tensor_tensor(normed[:, :, :].rearrange("p t (h w) -> p t h w", h=WIN),
                                    pv_win[:, :, :, 0:DH],
                                    recip[:, :].unsqueeze(2).unsqueeze(3).to_broadcast([P, RT, WIN, DH]),
                                    ALU.mult).then_inc(s["normed_done"], 1)

        def dve_unit(dve, b):
            k, u = b
            if present(("V", 0), k):
                dve_move_q(dve, b)
            if present(("A", 0), k):
                dve_norm(dve, b)
            for j in range(KT):
                if j == 1 and present(("K", 0), k):
                    dve_mask(dve, b)
                for slot in STEPS[j]:
                    if slot and present(slot, k):
                        if slot[0] == "K":
                            dve_k_lo(dve, b, slot[1])
                        elif slot[0] == "S":
                            dve_max(dve, b, slot[1])
            if present(("S", 0), k):
                dve_merge_max(dve, b)

        def pool_blocks(pool, b):
            k, u = b
            pool.wait_ge(s["normed_done"], k)
            if not known(k, 2):
                pool.wait_ge(s["attn_made"], k - 1)
            for t in range(RT):
                op = nc.gpsimd.tensor_tensor(blocks[:, t, DH * H0[t]:DH * (H0[t] + WIN)], normed[:, t, :],
                                             own[:, t, :], ALU.mult)
            op.then_inc(s["blocks_done"], 1)

        def pool_onehot(pool, b):
            k, u = b
            pool.wait_ge(s["any_done"], 2 * (k + 3))
            if not known(k, -1):
                pool.wait_ge(s["q_moved"], k + 2)
            if not known(k, 1):
                pool.wait_ge(s["blocks_done"], k)
            nc.gpsimd.tensor_tensor(q_stage[mr, :, :, :].rearrange("r p h q -> r (p h q)"), onehot[mr, :],
                                    any_key[mr, 0:1].to_broadcast([NR, PAIRS * QW]),
                                    ALU.mult).then_inc(s["onehot_placed"], 1)

        def pool_query(pool, b):
            k, u = b
            pool.wait_ge(s["onehot_placed"], k + 3)
            pool.wait_ge(s["q_copied"], k + 3)
            for h in range(2):
                def own_columns(c):
                    return parity[:, c:c + 1].unsqueeze(2).to_broadcast([64, PAIRS, S])
                nc.gpsimd.tensor_tensor(q_val[:, :, :], q_rows[:, :, :], own_columns(h), ALU.mult)
                nc.gpsimd.tensor_tensor(q_hi[:, :, :], q_rows[:, :, :], own_columns(2 + h), ALU.mult)\
                    .then_inc(s["q_step"], 1)
                pool.wait_ge(s["q_step"], 4 * (k + 2) + 2 * h + 1)
                nc.gpsimd.tensor_tensor(q_stage[0:64, :, h, :], q_val[:, :, :], q_hi[:, :, :],
                                        ALU.subtract).then_inc(s["q_step"], 1)
                pool.wait_ge(s["q_step"], 4 * (k + 2) + 2 * h + 2)

        def pool_unit(pool, b):
            k, u = b
            if present(("A", 0), k):
                pool_blocks(pool, b)
            if present(("Q", 0), k):
                pool_onehot(pool, b)
                pool_query(pool, b)

        def units(eng, unit):
            for k in (-2, -1, 0):
                unit(eng, (k, k % 2))
            with eng.Fori(1, B - 4, 2) as i:
                for v in range(2):
                    unit(eng, (eng.snap(i + v), 1 - v))
            for k in (B - 3, B - 2, B - 1):
                unit(eng, (k, k % 2))

        down_banks = [[ring[:, 0, :], ring[:, 1, :]], [ring[:, 2, :], pv[:, :]]]
        TILES = [range(0, 4), range(4, TT)]

        def sp_expert(sp, e, v):
            if e >= 2:
                sp.wait_ge(s["up_made"], HC * (e - 1))
            sp.dma_start(up_w[:, v, :], d["up_w"][bass.ds(e, 1), :, :].rearrange("e k i -> k (e i)"))\
                .then_inc(up_loaded[v], 16)
            if e >= 2:
                sp.wait_ge(s["down_made"], 2 * (e - 1))
            sp.dma_start(down_w[:, v, :, :],
                         d["down_w"][bass.ds(e, 1), :, :].rearrange("e (c i) h -> i (e c) h", c=HC))\
                .then_inc(down_loaded[v], 16)

        def pe_up(pe, e, v):
            pe.wait_ge(up_loaded[v], 8 * turn(e, v))
            for c in range(HC):
                if not isinstance(e, int) or 4 * e + c >= 2:
                    pe.wait_ge(s["hidden_done"], HC * e + c - 1)
                for h in range(2):
                    mm = nc.tensor.matmul(st[:, c % 2, h, 0:HALF], up_w[:, v, c * P:(c + 1) * P],
                                          xnT[:, h * HALF:(h + 1) * HALF], start=True, stop=True)
                mm.then_inc(s["up_made"], 1)

        def act_gelu(act, e, v):
            for c in range(HC):
                act.wait_ge(s["up_made"], HC * e + c + 1)
                if c == 0 and (not isinstance(e, int) or e >= 2):
                    act.wait_ge(s["down_made"], 2 * (e - 1))
                nc.scalar.activation(hidden[:, v, c, :].rearrange("p (h t) -> p h t", h=2),
                                     st[:, c % 2, :, 0:HALF], ACT.Gelu,
                                     bias=up_bias[:, bass.ds(e * HC + c, 1)]).then_inc(s["hidden_done"], 1)

        def pe_down(pe, e, v):
            pe.wait_ge(down_loaded[v], 8 * turn(e, v))
            pe.wait_ge(s["hidden_done"], HC * (e + 1))
            for h in range(2):
                if not isinstance(e, int) or e >= 2:
                    pe.wait_ge(s["mixed"], 2 * (e - 2) + h + 1)
                for i, t in enumerate(TILES[h]):
                    for c in range(HC):
                        mm = nc.tensor.matmul(down_banks[v][h][:, i * P:(i + 1) * P],
                                              hidden[:, v, c, t * P:(t + 1) * P], down_w[:, v, c, :],
                                              start=(c == 0), stop=(c == HC - 1))
                mm.then_inc(s["down_made"], 1)

        def dve_mix(dve, e, v):
            for h in range(2):
                dve.wait_ge(s["down_made"], 2 * e + h + 1)
                if not isinstance(e, int) or e >= 1:
                    dve.wait_ge(s["mixed"], 2 * (e - 1) + h + 1)
                for i, t in enumerate(TILES[h]):
                    op = nc.vector.scalar_tensor_tensor(out=acc[:, t, :], in0=down_banks[v][h][:, i * P:(i + 1) * P],
                                                        scalar=route[:, bass.ds(e, 1), t:t + 1]
                                                        .rearrange("p e t -> p (e t)"),
                                                        in1=acc[:, t, :], op0=ALU.mult, op1=ALU.add)
                op.then_inc(s["mixed"], 1)

        @block.sync
        def _(sp):
            sp.dma_start(xq[QA, :, :], d["x"][:, 0:QSPLIT, :].rearrange("b q d -> q b d")).then_inc(s["x_loaded"], 16)
            sp.dma_start(xq[QB, :, :], d["x"][:, QSPLIT:S, :].rearrange("b q d -> q b d")).then_inc(s["x_loaded"], 16)
            for i, w in enumerate(("qw", "kw", "vw", "ow")):
                sp.dma_start(w_raw[:, i, :], d[w]).then_inc(s["weights_loaded"], 16)
            sp.dma_start(ident[:, :], d["c_ident"]).then_inc(s["weights_loaded"], 16)
            sp_load_batch(sp, (0, 0))
            sp.dma_start(q_bias[mr, :], d["qb"].unsqueeze(0).to_broadcast([NR, D])).then_inc(s["consts_loaded"], 16)
            sp.dma_start(k_bias[:, :], d["kb"].unsqueeze(1)).then_inc(s["consts_loaded"], 16)
            sp.dma_start(v_bias[:, :], d["vb"].unsqueeze(1)).then_inc(s["consts_loaded"], 16)
            sp.dma_start(onehot[mr, :], d["c_onehot"]).then_inc(s["consts_loaded"], 16)
            sp.dma_start(skip[mr, :], d["c_skip"]).then_inc(s["weights_loaded"], 16)
            sp.dma_start(parity[:, :], d["c_parity"]).then_inc(s["consts_loaded"], 16)
            sp.dma_start(pick[:, :, :], d["c_pick"]).then_inc(s["consts_loaded"], 16)
            sp.dma_start(own[:, :, :], d["c_own"]).then_inc(s["consts_loaded"], 16)
            sp_load_batch(sp, (1, 1))
            sp.wait_ge(s["ones_set"], 1)
            sp.dma_start(x_tok[:, :, :], d["x"].rearrange("b q d -> (b q) d").rearrange("(t p) d -> p t d", p=P))\
                .then_inc(s["ffn_consts"], 16)
            sp.dma_start(o_bias[:, :], d["ob"].unsqueeze(0).to_broadcast([P, D])).then_inc(s["ffn_consts"], 16)
            sp.dma_start(gate_w[:, :], d["gate_w"]).then_inc(s["ffn_consts"], 16)
            sp.dma_start(gate_b[:, :], d["gate_b"].unsqueeze(0).to_broadcast([P, E])).then_inc(s["ffn_consts"], 16)
            sp.dma_start(up_b_raw[:, :], d["up_b"].rearrange("e (c i) -> (e c) i", c=HC)).then_inc(s["ffn_consts"], 16)
            sp.dma_start(down_b[:, :], d["down_b"]).then_inc(s["ffn_consts"], 16)
            sp.dma_start(rank[:, :], d["c_rank"]).then_inc(s["ffn_consts"], 16)
            sp.dma_start(gates[:, 0:1], d["gx"].unsqueeze(0).to_broadcast([P, 1])).then_inc(s["ffn_consts"], 16)
            sp.dma_start(gates[:, 1:2], d["gf"].unsqueeze(0).to_broadcast([P, 1])).then_inc(s["ffn_consts"], 16)
            sp_expert(sp, 0, 0)
            sp_expert(sp, 1, 1)

            units(sp, sp_unit)
            for e in range(2, NE):
                sp_expert(sp, e, e % 2)
            x_out = out.rearrange("b q d -> (b q) d").rearrange("(t p) d -> p t d", p=P)
            for h in range(2):
                sp.wait_ge(s["out_ready"], h + 1)
                t0, t1 = TILES[h][0], TILES[h][-1] + 1
                sp.dma_start(x_out[:, t0:t1, :], acc[:, t0:t1, :]).then_inc(s["out_stored"], 16)
            sp.wait_ge(s["out_stored"], 32)

        NFFN = 9
        NCONST = 7

        @block.scalar
        def _(act):
            act.wait_ge(s["w_turned"], 1)
            nc.scalar.activation(w_t[:, :, :].rearrange("p i d -> p (i d)"), ring[:, 0, :],
                                 ACT.Copy).then_inc(s["w_copied"], 1)
            act.wait_ge(s["stats_done"], 2 * B + 1)
            nc.scalar.activation(rstd[mr, :], rstd[mr, :], ACT.Sqrt).then_inc(s["rstd_var"], 1)
            act.wait_ge(s["ln_turned"], 1)
            nc.scalar.activation(lnT[:, 0:8 * NR], ring[:, 1, 0:8 * NR], ACT.Copy).then_inc(s["ln_copied"], 1)
            act.wait_ge(s["ln_turned"], 2)
            nc.scalar.activation(lnT[:, 8 * NR:16 * NR], ring[:, 2, 0:8 * NR], ACT.Copy).then_inc(s["ln_copied"], 1)
            act.wait_ge(s["consts_loaded"], 16 * NCONST)
            units(act, act_unit)
            act_attn(act, (B, 0))

            act.wait_ge(s["ffn_consts"], 16 * NFFN)
            nc.scalar.activation(tanh_g[:, :], gates[:, :], ACT.Tanh).then_inc(s["gates_tanh"], 1)
            act.wait_ge(s["ffn_var"], 2 * TT + 1)
            nc.scalar.activation(ln_rstd[:, :], ln_rstd[:, :], ACT.Sqrt).then_inc(s["ffn_ln_done"], 1)
            for h in range(2):
                w = P * len(TILES[h])
                act.wait_ge(s["xn_turned"], h + 1)
                nc.scalar.activation(xnT[:, 4 * P * h:4 * P * h + w], down_banks[1][h][:, 0:w],
                                     ACT.Copy).then_inc(s["xn_copied"], 1)
            act.wait_ge(s["bias_turned"], 1)
            nc.scalar.activation(up_bias[:, :], ring[:, 0, 0:NE * HC], ACT.Copy).then_inc(s["bias_copied"], 1)
            act.wait_ge(s["score_raw"], 1)
            nc.scalar.activation(score[:, :, :], score[:, :, :], ACT.Sigmoid).then_inc(s["score_done"], 1)
            act.wait_ge(s["bias_copied"], 1)
            for e in range(2):
                act_gelu(act, e, e)
            for h in range(2):
                w = P * len(TILES[h])
                act.wait_ge(s["route_turned"], h + 1)
                nc.scalar.activation(routeT[:, 4 * P * h:4 * P * h + w], down_banks[0][h][0:NE, 0:w],
                                     ACT.Copy).then_inc(s["route_copied"], 1)
            act_gelu(act, 2, 0)
            with act.Fori(3, NE - 1, 2) as i:
                for v in range(2):
                    act_gelu(act, act.snap(i + v), (1 + v) % 2)

        @block.tensor
        def _(pe):
            pe.wait_ge(s["weights_loaded"], 96)
            for i in range(4):
                mm = nc.tensor.transpose(ring[:, 0, i * P:(i + 1) * P], w_raw[:, i, :], ident[:, :])
            mm.then_inc(s["w_turned"], 1)
            for g in range(2):
                pe.wait_ge(s["ln_done"], B)
                for i in range(8):
                    b = 8 * g + i
                    mm = nc.tensor.matmul(ring[:, 1 + g, i * NR:(i + 1) * NR], xq[mr, b, :], ident[mr, mr],
                                          start=True, stop=True)
                mm.then_inc(s["ln_turned"], 1)
            pe.wait_ge(s["w_copied"], 1)
            for g in range(4):
                pe.wait_ge(s["ln_copied"], 1 + g // 2)
                for i in range(4):
                    b = 4 * g + i
                    mm = nc.tensor.matmul(st[mr, g // 2, g % 2, i * D:(i + 1) * D],
                                          lnT[:, b * NR:(b + 1) * NR], w_t[:, 0, :], start=True, stop=True)
                mm.then_inc(s["q_made"], 1)
            units(pe, pe_unit)
            pe_attn(pe, (B, 0))

            pe.wait_ge(s["attn_stored"], B)
            for h in range(2):
                for i, t in enumerate(TILES[h]):
                    mm = nc.tensor.matmul(down_banks[0][h][:, i * P:(i + 1) * P], attnT[:, t * P:(t + 1) * P],
                                          w_t[:, 3, :], start=True, stop=True)
                mm.then_inc(s["projected"], 1)
            for h in range(2):
                for i, t in enumerate(TILES[h]):
                    pe.wait_ge(s["ffn_var"], 2 * TT + 2 + t + 1)
                    if h == 1:
                        pe.wait_ge(s["normed_done"], B)
                    mm = nc.tensor.transpose(down_banks[1][h][:, i * P:(i + 1) * P], xn[:, t, :], ident[:, :])
                mm.then_inc(s["xn_turned"], 1)
            pe.wait_ge(s["x1_step"], 2)
            pe.wait_ge(s["ffn_consts"], 16 * NFFN)
            nc.tensor.transpose(ring[:, 0, 0:NE * HC], up_b_raw[:, :], ident[0:NE * HC, 0:NE * HC])\
                .then_inc(s["bias_turned"], 1)
            pe.wait_ge(s["xn_copied"], 2)
            for t in range(TT):
                mm = nc.tensor.matmul(ring[:, 1, t * E:(t + 1) * E], xnT[:, t * P:(t + 1) * P], gate_w[:, :],
                                      start=True, stop=True)
            mm.then_inc(s["gate_made"], 1)
            pe_up(pe, 0, 0)
            pe_up(pe, 1, 1)
            pe.wait_ge(s["route_done"], 1)
            pe.wait_ge(s["bias_copied"], 1)
            for h in range(2):
                for i, t in enumerate(TILES[h]):
                    mm = nc.tensor.transpose(down_banks[0][h][0:NE, i * P:(i + 1) * P], route[:, :, t], ident[:, :])
                mm.then_inc(s["route_turned"], 1)
            for h in range(2):
                pe.wait_ge(s["route_copied"], h + 1)
                for i, t in enumerate(TILES[h]):
                    mm = nc.tensor.matmul(down_banks[1][h][:, i * P:(i + 1) * P], routeT[:, t * P:(t + 1) * P],
                                          down_b[:, :], start=True, stop=True)
                mm.then_inc(s["bias_mixed"], 1)
            pe_down(pe, 0, 0)
            pe_up(pe, 2, 0)
            pe.wait_ge(s["acc_ready"], 2)
            pe_down(pe, 1, 1)
            with pe.Fori(2, NE - 2, 2) as i:
                for v in range(2):
                    e = pe.snap(i + v)
                    pe_up(pe, e + 1, (v + 1) % 2)
                    pe_down(pe, e, v)
            pe_down(pe, NE - 1, 0)

        @block.vector
        def _(dve):
            nc.vector.memset(xq[ONEROW:ONEROW + 1, :, :], 0.0).then_inc(s["dve_step"], 1)
            nc.vector.memset(mask_raw[ONEROW:ONEROW + 1, :, :], 1).then_inc(s["dve_step"], 1)
            nc.vector.memset(keys[96:P, :, :, :], 1.0).then_inc(s["ones_set"], 1)
            nc.vector.memset(v_ext[:, :, :, :, DH:VW], 1.0).then_inc(s["dve_step"], 1)
            dve.wait_ge(s["dve_step"], 3)
            dve.wait_ge(s["x_loaded"], 32)
            for b in range(B):
                nc.vector.bn_stats(stat[mr, b, :], xq[mr, b, :]).then_inc(s["stats_done"], 1)
            for b in range(B):
                dve.wait_ge(s["stats_done"], B if b == 0 else B + b)
                nc.vector.bn_aggr(mv[mr, b, :], stat[mr, b, :]).then_inc(s["stats_done"], 1)
            dve.wait_ge(s["stats_done"], 2 * B)
            nc.vector.tensor_scalar(rstd[mr, :], mv[mr, :, 1:2].rearrange("p b o -> p (b o)"), EPS, None,
                                    ALU.add).then_inc(s["stats_done"], 1)
            dve.wait_ge(s["rstd_var"], 1)
            nc.vector.reciprocal(rstd[mr, :], rstd[mr, :]).then_inc(s["rstd_done"], 1)
            dve.wait_ge(s["rstd_done"], 1)
            for b in range(B):
                nc.vector.tensor_scalar(xq[mr, b, :], xq[mr, b, :], mv[mr, b, 0:1], rstd[mr, b:b + 1],
                                        ALU.subtract, ALU.mult).then_inc(s["ln_done"], 1)
            dve.wait_ge(s["consts_loaded"], 16 * NCONST)
            for g in range(4):
                dve.wait_ge(s["q_made"], g + 1)
                nc.vector.tensor_tensor(q_all[mr, 4 * g:4 * g + 4, :],
                                        st[mr, g // 2, g % 2, :].rearrange("q (b d) -> q b d", b=4),
                                        q_bias[mr, :].unsqueeze(1).to_broadcast([NR, 4, D]), ALU.add)\
                    .then_inc(s["dve_step"], 1)
            dve.wait_ge(s["dve_step"], 7)
            nc.vector.tensor_scalar(q_all[mr, :, :], q_all[mr, :, :], float(DH) ** -0.5, None,
                                    ALU.mult).then_inc(s["q_stored"], 1)
            units(dve, dve_unit)
            dve_norm(dve, (B, 0))

            dve.wait_ge(s["gates_tanh"], 1)
            for h in range(2):
                t0, t1 = TILES[h][0], TILES[h][-1] + 1
                dve.wait_ge(s["projected"], h + 1)
                nc.vector.tensor_tensor(xn[:, t0:t1, :],
                                        down_banks[0][h][:, 0:(t1 - t0) * P].rearrange("p (t d) -> p t d", d=D),
                                        o_bias[:, :].unsqueeze(1).to_broadcast([P, t1 - t0, D]),
                                        ALU.add).then_inc(s["x1_step"], 1)
            for h in range(2):
                t0, t1 = TILES[h][0], TILES[h][-1] + 1
                dve.wait_ge(s["x1_step"], h + 1)
                nc.vector.scalar_tensor_tensor(out=x_tok[:, t0:t1, :], in0=xn[:, t0:t1, :], scalar=tanh_g[:, 0:1],
                                               in1=x_tok[:, t0:t1, :], op0=ALU.mult,
                                               op1=ALU.add).then_inc(s["x1_done"], 1)
            for t in range(TT):
                if t in (0, 4):
                    dve.wait_ge(s["x1_done"], 1 + t // 4)
                nc.vector.bn_stats(ln_stat[:, t, :], x_tok[:, t, :]).then_inc(s["ffn_var"], 1)
            dve.wait_ge(s["ffn_var"], TT)
            for t in range(TT):
                nc.vector.bn_aggr(ln_mv[:, t, :], ln_stat[:, t, :]).then_inc(s["ffn_var"], 1)
            dve.wait_ge(s["ffn_var"], 2 * TT)
            nc.vector.tensor_scalar(ln_rstd[:, :], ln_mv[:, :, 1:2].rearrange("p t o -> p (t o)"), EPS, None,
                                    ALU.add).then_inc(s["ffn_var"], 1)
            dve.wait_ge(s["ffn_ln_done"], 1)
            nc.vector.reciprocal(ln_rstd[:, :], ln_rstd[:, :]).then_inc(s["ffn_var"], 1)
            dve.wait_ge(s["ffn_var"], 2 * TT + 2)
            for t in range(TT):
                nc.vector.tensor_scalar(xn[:, t, :], x_tok[:, t, :], ln_mv[:, t, 0:1], ln_rstd[:, t:t + 1],
                                        ALU.subtract, ALU.mult).then_inc(s["ffn_var"], 1)

            dve.wait_ge(s["gate_made"], 1)
            nc.vector.tensor_tensor(score[:, :, :], ring[:, 1, 0:TT * E].rearrange("p (t e) -> p t e", e=E),
                                    gate_b[:, :].unsqueeze(1).to_broadcast([P, TT, E]),
                                    ALU.add).then_inc(s["score_raw"], 1)
            dve.wait_ge(s["score_done"], 1)
            steps = [0]

            def then(op):
                op.then_inc(s["route_step"], 1)
                steps[0] += 1
                dve.wait_ge(s["route_step"], steps[0])

            def over_experts(v):
                return v.unsqueeze(2).to_broadcast([P, TT, E])

            rank3 = rank[:, :].rearrange("p (t e) -> p t e", e=E)
            then(nc.vector.memset(route[:, E, :], 1.0))
            for r, chosen in enumerate((pick1, pick2)):
                then(nc.vector.tensor_reduce(topv[:, r, :], score[:, :, :], AX.X, ALU.max))
                then(nc.vector.tensor_tensor(tmp[:, :, :], score[:, :, :], over_experts(topv[:, r, :]), ALU.is_equal))
                then(nc.vector.tensor_tensor(tmp[:, :, :], tmp[:, :, :], rank3, ALU.mult))
                then(nc.vector.tensor_reduce(tmpv[:, :], tmp[:, :, :], AX.X, ALU.max))
                then(nc.vector.tensor_tensor(chosen[:, :, :], tmp[:, :, :], over_experts(tmpv[:, :]), ALU.is_equal))
                if r == 0:
                    then(nc.vector.scalar_tensor_tensor(out=score[:, :, :], in0=chosen[:, :, :], scalar=-4.0,
                                                        in1=score[:, :, :], op0=ALU.mult, op1=ALU.add))
            then(nc.vector.scalar_tensor_tensor(out=tmpv[:, :], in0=topv[:, 0, :], scalar=1e-6, in1=topv[:, 1, :],
                                                op0=ALU.add, op1=ALU.add))
            then(nc.vector.reciprocal(tmpv[:, :], tmpv[:, :]))
            for r, chosen in enumerate((pick1, pick2)):
                then(nc.vector.tensor_tensor(topv[:, r, :], topv[:, r, :], tmpv[:, :], ALU.mult))
                then(nc.vector.tensor_tensor(chosen[:, :, :], chosen[:, :, :], over_experts(topv[:, r, :]), ALU.mult))
            nc.vector.tensor_tensor(route[:, 0:E, :].rearrange("p e t -> p t e"), pick1[:, :, :], pick2[:, :, :],
                                    ALU.add).then_inc(s["route_done"], 1)
            for h in range(2):
                t0, t1 = TILES[h][0], TILES[h][-1] + 1
                dve.wait_ge(s["bias_mixed"], h + 1)
                nc.vector.tensor_copy(acc[:, t0:t1, :].rearrange("p t d -> p (t d)"),
                                      down_banks[1][h][:, 0:(t1 - t0) * P]).then_inc(s["acc_ready"], 1)
            dve.wait_ge(s["acc_ready"], 2)
            dve.wait_ge(s["route_done"], 1)
            dve_mix(dve, 0, 0)
            dve_mix(dve, 1, 1)
            with dve.Fori(2, NE - 2, 2) as i:
                for v in range(2):
                    dve_mix(dve, dve.snap(i + v), v)
            dve_mix(dve, NE - 1, 0)
            dve.wait_ge(s["mixed"], 2 * NE)
            nc.vector.tensor_reduce(tmpv[:, :], acc[:, :, :], AX.X, ALU.max,
                                    apply_absolute_value=True).then_inc(s["out_step"], 1)
            dve.wait_ge(s["out_step"], 1)
            nc.vector.tensor_scalar(tmpv[:, :], tmpv[:, :], 0.1, 1e-6, ALU.mult, ALU.add).then_inc(s["out_step"], 1)
            dve.wait_ge(s["out_step"], 2)
            nc.vector.reciprocal(tmpv[:, :], tmpv[:, :]).then_inc(s["out_step"], 1)
            dve.wait_ge(s["out_step"], 3)
            nc.vector.tensor_scalar(tmpv[:, :], tmpv[:, :], tanh_g[:, 1:2], 0.1, ALU.mult,
                                    ALU.mult).then_inc(s["out_step"], 1)
            dve.wait_ge(s["out_step"], 4)
            for h in range(2):
                for t in TILES[h]:
                    op = nc.vector.scalar_tensor_tensor(out=acc[:, t, :], in0=acc[:, t, :], scalar=tmpv[:, t:t + 1],
                                                        in1=x_tok[:, t, :], op0=ALU.mult, op1=ALU.add)
                op.then_inc(s["out_ready"], 1)

        @block.gpsimd
        def _(pool):
            nc.gpsimd.memset(blocks[:, :, :], 0.0).then_inc(s["blocks_zeroed"], 1)
            pool.wait_ge(s["blocks_zeroed"], 1)
            pool.wait_ge(s["consts_loaded"], 16 * NCONST)
            pool.wait_ge(s["q_stored"], 1)
            units(pool, pool_unit)
            pool_blocks(pool, (B, 0))


_INS = {
    "x": "x", "ctx": "ctx_1024", "mask": "mask_BxSxS2_if1", "gx": "g_xattn", "gf": "g_ffn",
    "qw": "L0_xattn_qw", "qb": "L0_xattn_qb", "kw": "L0_xattn_kw", "kb": "L0_xattn_kb",
    "vw": "L0_xattn_vw", "vb": "L0_xattn_vb", "ow": "L0_xattn_ow", "ob": "L0_xattn_ob",
    "gate_w": "L0_ffn_gate_w", "gate_b": "L0_ffn_bias",
}


def kernel(**inputs):
    import concourse.bacc as _bacc
    from concourse.bass_utils import run_bass_kernel_spmd as _run

    arrays = {k: np.ascontiguousarray(inputs[v]) for k, v in _INS.items()}
    for k, routed, shared in (("up_w", "L0_ffn_up_w", "L0_ffn_sw_up"), ("up_b", "L0_ffn_up_b", "L0_ffn_sb_up"),
                              ("down_w", "L0_ffn_down_w", "L0_ffn_sw_down"),
                              ("down_b", "L0_ffn_down_b", "L0_ffn_sb_down")):
        arrays[k] = np.concatenate([np.asarray(inputs[routed]), np.asarray(inputs[shared])[None]])
    arrays.update(constants())
    nc = _bacc.Bacc("TRN2", target_bir_lowering=False, num_devices=1)
    feeds, aps = {}, {}
    for k, a in arrays.items():
        feeds["in_" + k] = a
        aps[k] = nc.dram_tensor("in_" + k, a.shape, mybir.dt.from_np(a.dtype), kind="ExternalInput").ap()
    out = nc.dram_tensor("out_0", (B, S, D), F32, kind="ExternalOutput").ap()
    flamingo_kernel(nc, aps, out)
    r = _run(nc, [feeds], core_ids=[0])
    return r.results[0]["out_0"]
```

```python
from contextlib import ExitStack

import numpy as np
import concourse.bass as bass
from concourse import mybir

ALU = mybir.AluOpType
ACT = mybir.ActivationFunctionType
F32 = mybir.dt.float32
F16 = mybir.dt.float16
I32 = mybir.dt.int32
AX = mybir.AxisListType

P = 128
B, S, D, H = 16, 56, 128, 16
DH = D // H
NK = 1500
KT = 12
KLAST = NK - (KT - 1) * P
PAIRS = H // 2
QW = 2 * S
HQ = H * S
RT = HQ // P
TOK = B * S
TT = TOK // P
MROW = 64
ONEROW = 96
QSPLIT = ONEROW - MROW
NR = S + 1
ROWS = MROW + NR
NCH = 3
CH = 512
VW = 2 * DH + 1
V_SCALE = 16.0
P_SCALE = 256.0
WIN = 4
H0 = [min(P * t // S, H - WIN) for t in range(RT)]
BIG = 32768.0
E = 8
NE = E + 1
HID = 4 * D
HC = HID // P
EPS = 1e-5
HALF = TOK // 2
W_SCALE = 64.0
H_SCALE = 64.0


def constants():
    row = np.arange(HQ).reshape(RT, P)
    head, query = row // S, row % S
    pick = (query[:, :, None] == np.arange(S)).transpose(1, 0, 2).astype(np.float32)
    own = (head[:, :, None] == (np.array(H0)[:, None] + np.arange(WIN))[:, None, :])
    own = np.repeat(own.transpose(1, 0, 2)[..., None], DH, axis=3).reshape(P, RT, WIN * DH)
    skip = np.insert(np.eye(S, dtype=np.float32), QSPLIT, 0.0, axis=0)
    onehot = np.tile(skip.astype(np.float16) * np.float16(BIG), (1, 2 * PAIRS))
    rank = np.tile(np.arange(E, 0, -1, dtype=np.float32), (P, TT))
    return {
        "c_ident": np.eye(P, dtype=np.float32),
        "c_pick": pick,
        "c_own": (own / V_SCALE).astype(np.float32),
        "c_skip": skip,
        "c_onehot": onehot,
        "c_rank": rank,
    }


def flamingo_kernel(nc, d, out):
    with ExitStack() as ctx:
        def sb(name, shape, dt=F32):
            return ctx.enter_context(nc.sbuf_tensor(name, shape, dt))

        def sem(name):
            return ctx.enter_context(nc.semaphore(name))

        ident = sb("ident", [P, P])
        pick = sb("pick", [P, RT, S])
        skip = sb("skip", [P, S])
        own = sb("own", [P, RT, WIN * DH])
        rank = sb("rank", [P, TT * E])
        w_raw = sb("w_raw", [P, 4, D])
        w_t = sb("w_t", [P, 4, D])
        q_bias = sb("q_bias", [P, D])
        k_bias = sb("k_bias", [P, 1])
        v_bias = sb("v_bias", [P, 1])
        gates = sb("gates", [P, 2])
        tanh_g = sb("tanh_g", [P, 2])
        lnT = sb("lnT", [P, B * NR])
        q_all = sb("q_all", [P, B, D])
        q_any = sb("q_any", [P, PAIRS, 2, 4, 2 * DH])
        q_hi = sb("q_hi", [64, 2, 4 * QW], F16)
        mask_raw = sb("mask_raw", [P, 2, NK], I32)
        mask_abs = sb("mask_abs", [P, 2])
        any_key = sb("any_key", [P, 1])
        fill = sb("fill", [P, 1])
        mask_add = sb("mask_add", [P, NK], F16)
        ctx_raw = sb("ctx_raw", [P, 2, KT, D])
        ctxT = sb("ctxT", [P, NK])
        k_hi = sb("k_hi", [P, NK], F16)
        k_lo = sb("k_lo", [P, NK], F16)
        keys = sb("keys", [P, 2, PAIRS, NK], F16)
        qrs = sb("qrs", [P, 2, PAIRS, 2, S], F16)
        ones_row = sb("ones_row", [1, NK], F16)
        q_stage = sb("q_stage", [P, PAIRS, 2, S], F16)
        v_ext = sb("v_ext", [P, 2, KT, H, VW], F16)
        pv_sum = sb("pv_sum", [P, RT * WIN, DH])
        p_hi = sb("p_hi", [P, 3, HQ], F16)
        p_lo = sb("p_lo", [P, 3, HQ], F16)
        p_scale = sb("p_scale", [P, 1])
        lo_row = sb("lo_row", [64, 1])
        max_part = sb("max_part", [QW, PAIRS, NCH])
        neg_max = sb("neg_max", [QW, PAIRS])
        probs = sb("probs", [P, 3, HQ])
        recip = sb("recip", [P, RT])
        normed = sb("normed", [P, RT, WIN * DH])
        blocks = sb("blocks", [P, RT, D])
        attnT = sb("attnT", [P, TOK])

        x_tok = sb("x_tok", [P, TT, D])
        o_bias = sb("o_bias", [P, D])
        gate_w = sb("gate_w", [P, E])
        gate_b = sb("gate_b", [P, E])
        up_b_raw = sb("up_b_raw", [NE * HC, P])
        up_bias = sb("up_bias", [P, NE * HC])
        down_b = sb("down_b", [NE, D])
        down_bs = sb("down_bs", [NE, D])
        up_w = sb("up_w", [P, 2, HID])
        down_w = sb("down_w", [P, 2, HC, D])
        ln_stat = sb("ln_stat", [P, TT, 6])
        ln_mv = sb("ln_mv", [P, TT, 2])
        ln_rstd = sb("ln_rstd", [P, TT])
        xn = sb("xn", [P, TT, D])
        xnT = lnT[:, 0:TOK]
        score = sb("score", [P, TT, E])
        topv = sb("topv", [P, 2, TT])
        pick1 = sb("pick1", [P, TT, E])
        pick2 = sb("pick2", [P, TT, E])
        tmp = sb("tmp", [P, TT, E])
        tmpv = sb("tmpv", [P, TT])
        route = sb("route", [P, NE, TT])
        routeT = sb("routeT", [NE, TOK])
        acc = sb("acc", [P, TT, D])
        spent, at = keys[:, :, :, :].rearrange("p u a k -> p (u a k)"), 0
        hid = spent[:, at:at + 4 * HC * TOK].rearrange("p (v x c t) -> p v x c t", v=2, x=2, c=HC)
        at += 4 * HC * TOK
        up_p = spent[:, at:at + 4 * HID].rearrange("p (v x n) -> p v x n", v=2, x=2)
        at += 4 * HID
        down_p = spent[:, at:at + 4 * HID].rearrange("p (v x n) -> p v x n", v=2, x=2)
        at += 4 * HID
        xn_p = spent[:, at:at + 2 * TOK].rearrange("p (x t) -> p x t", x=2)
        at += 2 * TOK
        w_all = spent[:, at:at + 4 * TOK].bitcast(F32).rearrange("p (v t) -> p v t", v=2)
        hid_raw = [probs[:, c, :] for c in range(HC - 1)] + \
            [ctx_raw[:, :, :, :].rearrange("p u t d -> p (u t d)")[:, 0:TOK]]

        route_dram = nc.dram_tensor("route_dram", (NE, TOK), F32, kind="Internal").ap()
        k_dram = nc.dram_tensor("k_dram", (2, P, NK), F16, kind="Internal").ap()
        ring = ctx.enter_context(nc.psum_tensor("ring", [P, 3, 512], F32))
        st = ctx.enter_context(nc.psum_tensor("st", [P, 2, 2, 512], F32))
        pv = ctx.enter_context(nc.psum_tensor("pv", [P, 512], F32))
        pv_win = pv[:, 0:RT * WIN * VW].rearrange("p (t h w) -> p t h w", t=RT, h=WIN)

        names = """
        consts_loaded weights_loaded x_loaded k_spilled ones_set
        w_turned w_copied ln_stats ln_var ln_done ln_gap ln_turned ln_copied q_made q_stored
        ctx_turned ctx_copied k_made k_hi_stored k_lo_stored v_made v_stored
        mask_abs_done any_done fill_done mask_ready q_blanked q_spread q_hi_done q_built
        blocks_zeroed v_hi_stored p_hi_done p_hi_cast
        p_lo_done sums_read ones_placed
        q_moved scored max_read max_merged max_turned max_copied
        st_made exps_done pv_done recip_done normed_done blocks_done attn_made attn_stored dve_step
        ffn_consts gates_tanh projected x1_step x1_done ffn_stats ffn_var ffn_ln_done xn_turned xn_copied bias_turned
        bias_copied gate_made score_raw score_done route_step route_done route_turned route_copied
        up_made gelu_done weighted hid_hi_done hid_lo_done down_made up_hi_split up_split down_hi_split down_split
        down_b_scaled xn_hi_done xn_split route_stored mixed mix_copied mix_turned out_step out_ready out_stored
        """.split()
        s = {n: sem("s_" + n) for n in names}
        ctx_loaded = [sem(f"s_ctx_loaded{u}") for u in range(2)]
        mask_loaded = [sem(f"s_mask_loaded{u}") for u in range(2)]
        up_loaded = [sem(f"s_up_loaded{u}") for u in range(2)]
        w_all_loaded = [sem(f"s_w_all_loaded{u}") for u in range(2)]
        down_loaded = [sem(f"s_down_loaded{u}") for u in range(2)]

        def turn(k, u):
            return k - u + 2

        keys_placed = [sem(f"s_keys_placed{c}") for c in range(NCH)]

        block = ctx.enter_context(nc.Block())

        mr = slice(MROW, ROWS)
        QA, QB = slice(MROW, ONEROW), slice(ONEROW + 1, ROWS)


        def known(k, below):
            return isinstance(k, int) and k < below

        def tile_keys(j):
            return P if j < KT - 1 else KLAST

        def chunk(c):
            return slice(c * CH, min((c + 1) * CH, NK))

        STEPS, done = [], 0
        for step in ("S V0 S", "S V1 T0 S", "S V2 T1 S", "S T2 K0 S S",
                     "S K1 S", "K2", "S A0 S S S", "S Q0",
                     "S Q1 S S", "S S S", "S S", "M0 M1 -"):
            slots = []
            for slot in step.split():
                slots.append(None if slot == "-" else ("S", done) if slot == "S" else (slot[0], int(slot[1])))
                done += slot == "S"
            STEPS.append(slots)
        K_STEP = STEPS.index(next(step for step in STEPS if ("K", 0) in step))
        Q_STEP = STEPS.index(next(step for step in STEPS if ("Q", 0) in step))
        ORDER = [slot for step in STEPS for slot in step]
        assert done == PAIRS * NCH and len(ORDER) % 3 == 0
        RING = {slot: i % 3 for i, slot in enumerate(ORDER) if slot}
        KIND = {"V": (1, NCH, "v_stored"), "T": (2, NCH, "ctx_copied"), "K": (2, NCH, "k_lo_stored"),
                "Q": (2, 2, "q_built"), "A": (-1, 1, "attn_stored"), "S": (1, PAIRS * NCH, "max_read"),
                "M": (1, 2, "max_copied")}

        def present(slot, k):
            off = KIND[slot[0]][0]
            return not isinstance(k, int) or 0 <= k + off < B

        def ring_free(pe, k, slot):
            i = ORDER.index(slot)
            while True:
                i -= 3
                if i < 0:
                    i, k = i + len(ORDER), k - 1
                if known(k, -2):
                    return
                if ORDER[i] and present(ORDER[i], k):
                    off, count, name = KIND[ORDER[i][0]]
                    pe.wait_ge(s[name], count * (k + off) + ORDER[i][1] + 1)
                    return

        def sp_load_batch(sp, n):
            k, u = n
            src = d["ctx"][bass.ds(k, 1), :, :]
            sp.dma_start(ctx_raw[:, u, 0:KT - 1, :],
                         src[:, 0:(KT - 1) * P, :].rearrange("b (t p) d -> p (b t) d", p=P)).then_inc(ctx_loaded[u], 16)
            sp.dma_start(ctx_raw[0:KLAST, u, KT - 1, :],
                         src[:, (KT - 1) * P:NK, :].rearrange("b p d -> p (b d)")).then_inc(ctx_loaded[u], 16)
            msk = d["mask"][bass.ds(k, 1), :, :].rearrange("b q k -> q (b k)")
            sp.dma_start(mask_raw[QA, u, :], msk[0:QSPLIT, :]).then_inc(mask_loaded[u], 16)
            sp.dma_start(mask_raw[QB, u, :], msk[QSPLIT:S, :]).then_inc(mask_loaded[u], 16)

        def sp_place(sp, n, c):
            k, u = n
            if not known(k, 2):
                sp.wait_ge(s["st_made"], KT * (k - 2) + 4 * (c + 1))
            for rows in (QA, QB):
                nq = rows.stop - rows.start
                sp.dma_start(keys[rows, u, :, chunk(c)],
                             mask_add[rows, chunk(c)].unsqueeze(1).to_broadcast([nq, PAIRS, chunk(c).stop - c * CH]))\
                    .then_inc(keys_placed[c], 16)
            if c == 0:
                sp.wait_ge(s["k_spilled"], 32 * (k + 1))
            for r in range(4):
                sp.dma_start(keys[16 * r:16 * r + 16, u, :, chunk(c)],
                             k_dram[r % 2, :, chunk(c)].rearrange("(p i) k -> i p k", i=16))\
                    .then_inc(keys_placed[c], 16)

        def sp_unit(sp, b):
            k, u = b
            n = (k + 2, u)
            if not known(k, -2) and not (isinstance(k, int) and k + 2 >= B):
                sp.wait_ge(s["k_lo_stored"], NCH * (k + 3))
                sp.dma_start(k_dram[0], k_hi[:, :]).then_inc(s["k_spilled"], 16)
                sp.dma_start(k_dram[1], k_lo[:, :]).then_inc(s["k_spilled"], 16)
                if not (isinstance(k, int) and (k + 3 >= B or k + 3 < 2)):
                    sp_load_batch(sp, (k + 3, 1 - u))
                if known(k, -1):
                    sp.wait_ge(s["mask_ready"], 1)
                    sp.wait_ge(s["ones_set"], 4)
                    sp.dma_start(keys[ONEROW:ONEROW + 1, :, :, :].rearrange("r u p k -> r (u p) k"),
                                 ones_row[:, :].unsqueeze(1).to_broadcast([1, 2 * PAIRS, NK]))\
                        .then_inc(s["ones_placed"], 16)
                for c in range(NCH):
                    sp_place(sp, n, c)

        def pe_ctx_turn(pe, b, c):
            k, u = b
            ring_free(pe, k, ("T", c))
            if c == 0:
                pe.wait_ge(ctx_loaded[u], 16 * turn(k + 2, u))
            for i in range(4):
                j = 4 * c + i
                m = tile_keys(j)
                mm = nc.tensor.transpose(ring[:, RING[("T", c)], i * P:i * P + m],
                                         ctx_raw[0:m, u, j, :], ident[0:m, 0:m])
            mm.then_inc(s["ctx_turned"], 1)

        def pe_k(pe, b, c):
            k, u = b
            ring_free(pe, k, ("K", c))
            pe.wait_ge(s["ctx_copied"], NCH * (k + 2) + c + 1)
            w = chunk(c).stop - c * CH
            nc.tensor.matmul(ring[:, RING[("K", c)], 0:w], w_t[:, 1, :], ctxT[:, chunk(c)],
                             start=True, stop=True).then_inc(s["k_made"], 1)

        def pe_v(pe, b, c):
            k, u = b
            ring_free(pe, k, ("V", c))
            for i in range(4):
                j = 4 * c + i
                m = tile_keys(j)
                mm = nc.tensor.matmul(ring[0:m, RING[("V", c)], i * P:(i + 1) * P], ctxT[:, j * P:j * P + m],
                                      w_t[:, 2, :], start=True, stop=True)
            mm.then_inc(s["v_made"], 1)

        def pe_q_waits(pe, b, g):
            ring_free(pe, b[0], ("Q", g))
            pe.wait_ge(s["q_blanked"], 2 * (b[0] + 3))

        def pe_q(pe, b, g):
            bank = ring[0:64, RING[("Q", g)], 0:4 * QW].rearrange("r (p h q) -> r p h q", p=4, h=2)
            for i in range(4):
                for h in range(2):
                    mm = nc.tensor.matmul(bank[:, i, h, :], q_any[mr, 4 * g + i, h, :, :].rearrange("q r d -> q (r d)"),
                                          skip[mr, :], start=True, stop=True)
            mm.then_inc(s["q_spread"], 1)

        def pe_score(pe, b, m):
            k, u = b
            c, p = divmod(m, PAIRS)
            w = chunk(c).stop - c * CH
            ring_free(pe, k, ("S", m))
            if m == 0:
                pe.wait_ge(s["q_moved"], k + 2)
            if p == 0:
                pe.wait_ge(keys_placed[c], 96 * (k + 2))
            nc.tensor.matmul(ring[0:QW, RING[("S", m)], 0:w],
                             qrs[0:ROWS, 1 - u, p, :, :].rearrange("r h q -> r (h q)"),
                             keys[0:ROWS, 1 - u, p, chunk(c)], start=True, stop=True).then_inc(s["scored"], 1)

        def pe_max_row(pe, b, g):
            k, u = b
            ring_free(pe, k, ("M", g))
            if g == 0:
                pe.wait_ge(s["max_merged"], k + 2)
            for i in range(4):
                mm = nc.tensor.matmul(ring[ONEROW:ONEROW + 1, RING[("M", g)], i * QW:(i + 1) * QW],
                                      neg_max[:, 4 * g + i:4 * g + i + 1], ident[0:QW, 0:QW], start=True, stop=True)
            mm.then_inc(s["max_turned"], 1)

        CAST = (10,)

        def hi_count(j, by_cast):
            return sum((i in CAST) == by_cast for i in range(j + 1))

        def wait_st_read(eng, k, j):
            if j < 0:
                j, k = j + KT, k - 1
            if j in CAST:
                eng.wait_ge(s["exps_done"], KT * k + j + 1)
            else:
                eng.wait_ge(s["p_hi_done"], (KT - len(CAST)) * k + hi_count(j, False))

        def pe_scores_t(pe, b, j):
            k, u = b
            m = tile_keys(j)
            if j == 0:
                pe.wait_ge(s["max_copied"], 2 * (k + 1))
            if j >= 2 or not known(k, 1):
                wait_st_read(pe, k, j - 2)
            for p in range(PAIRS):
                mm = nc.tensor.matmul(st[0:m, j % 2, p // 4, QW * (p % 4):QW * (p % 4 + 1)],
                                      keys[0:ROWS, u, p, j * P:j * P + m],
                                      qrs[0:ROWS, u, p, :, :].rearrange("r h q -> r (h q)"),
                                      start=True, stop=True)
            mm.then_inc(s["st_made"], 1)

        def pe_pv(pe, b, j):
            k, u = b
            m = tile_keys(j)
            pe.wait_ge(s["p_lo_done"], KT * k + j + 1)
            if j == 0:
                pe.wait_ge(s["v_stored"], NCH * (k + 1))
                if not known(k, 1):
                    pe.wait_ge(s["sums_read"], k)
            for t in range(RT):
                for part in (p_hi, p_lo):
                    mm = nc.tensor.matmul(pv_win[:, t, :, :].rearrange("p h w -> p (h w)"),
                                          part[0:m, j % 3, t * P:(t + 1) * P],
                                          v_ext[0:m, u, j, H0[t]:H0[t] + WIN, :].rearrange("p h w -> p (h w)"),
                                          start=(j == 0 and t == 0 and part is p_hi),
                                          stop=(j == KT - 1 and part is p_lo), skip_group_check=True)
            mm.then_inc(s["pv_done"], 1)

        def pe_attn(pe, b):
            k, u = b
            if known(-k if isinstance(k, int) else k, -B + 1):
                pe.wait_ge(s["attn_stored"], B - 1)
            else:
                ring_free(pe, k, ("A", 0))
            pe.wait_ge(s["blocks_done"], k)
            for t in range(RT):
                mm = nc.tensor.matmul(ring[:, RING[("A", 0)], 0:S], blocks[:, t, :], pick[:, t, :],
                                      start=(t == 0), stop=(t == RT - 1))
            mm.then_inc(s["attn_made"], 1)

        PE_SLOT = {"T": pe_ctx_turn, "K": pe_k, "V": pe_v, "S": pe_score, "M": pe_max_row,
                   "Q": pe_q, "A": lambda pe, b, c: pe_attn(pe, b)}

        def attends(k):
            return not isinstance(k, int) or k >= 0

        LAG = 2

        def pe_unit(pe, b, steps=range(KT)):
            k, u = b
            for j in steps:
                if attends(k):
                    pe_scores_t(pe, b, j)
                for g in range(2):
                    if ("Q", g) in STEPS[j] and present(("Q", g), k):
                        pe_q_waits(pe, b, g)
                for slot in STEPS[j]:
                    if slot and present(slot, k):
                        PE_SLOT[slot[0]](pe, b, slot[1])
                if j >= LAG and attends(k):
                    pe_pv(pe, b, j - LAG)
                if j < LAG and attends(k - 1) and not known(k, 1):
                    pe_pv(pe, (k - 1, 1 - u), KT - LAG + j)

        def act_ctx(act, b, c):
            k, u = b
            act.wait_ge(s["ctx_turned"], NCH * (k + 2) + c + 1)
            if not known(k, -1):
                act.wait_ge(s["v_made"], NCH * (k + 1) + c + 1)
            w = chunk(c).stop - c * CH
            nc.scalar.activation(ctxT[:, chunk(c)], ring[:, RING[("T", c)], 0:w],
                                 ACT.Copy).then_inc(s["ctx_copied"], 1)

        def act_k_hi(act, b, c):
            k, u = b
            act.wait_ge(s["k_made"], NCH * (k + 2) + c + 1)
            if c == 0 and not known(k, -1):
                for x in keys_placed:
                    act.wait_ge(x, 96 * (k + 2))
            w = chunk(c).stop - c * CH
            nc.scalar.activation(k_hi[:, chunk(c)], ring[:, RING[("K", c)], 0:w], ACT.Identity,
                                 bias=k_bias[:, 0:1]).then_inc(s["k_hi_stored"], 1)

        def v_parts(b, c):
            v = 1 - b[1]
            src = ring[:, RING[("V", c)], :].rearrange("p (n w) -> p n w", w=DH)
            full = 4 if c < NCH - 1 else 3
            dst = v_ext[:, v, 4 * c:4 * c + full, :, :].rearrange("p i h w -> p (i h) w")
            out_ = [(src[:, 0:full * H, :], dst)]
            if c == NCH - 1:
                out_.append((src[0:KLAST, 3 * H:4 * H, :], v_ext[0:KLAST, v, KT - 1, :, :]))
            return out_

        def act_v(act, b, c):
            k, u = b
            act.wait_ge(s["v_made"], NCH * (k + 1) + c + 1)
            if not known(k, 1):
                act.wait_ge(s["pv_done"], KT * (k - 1) + 4 * (c + 1))
            for src, dst in v_parts(b, c):
                op = nc.scalar.activation(dst[:, :, 0:DH], src, ACT.Copy, scale=V_SCALE)
            op.then_inc(s["v_hi_stored"], 1)

        def act_q_hi(act, b, g):
            k, u = b
            act.wait_ge(s["q_spread"], 2 * (k + 2) + g + 1)
            if not known(k, -1):
                act.wait_ge(s["q_built"], 2 * (k + 1) + g + 1)
            nc.scalar.activation(q_hi[:, g, :], ring[0:64, RING[("Q", g)], 0:4 * QW], ACT.Copy,
                                 scale=lo_row[:, 0:1]).then_inc(s["q_hi_done"], 1)

        def act_attn(act, b):
            k, u = b
            act.wait_ge(s["attn_made"], k)
            nc.scalar.activation(attnT[:, bass.ds((k - 1) * S, S)], ring[:, RING[("A", 0)], 0:S], ACT.Identity,
                                 bias=v_bias[:, 0:1]).then_inc(s["attn_stored"], 1)

        def act_max_row(act, b, g):
            k, u = b
            act.wait_ge(s["max_turned"], 2 * (k + 1) + g + 1)
            nc.scalar.activation(qrs[ONEROW:ONEROW + 1, 1 - u, 4 * g:4 * g + 4, :, :].rearrange("r p h q -> r (p h q)"),
                                 ring[ONEROW:ONEROW + 1, RING[("M", g)], 0:4 * QW],
                                 ACT.Copy).then_inc(s["max_copied"], 1)

        def act_exp(act, b, j):
            k, u = b
            m = tile_keys(j)
            act.wait_ge(s["st_made"], KT * k + j + 1)
            if j >= 3 or not known(k, 1):
                act.wait_ge(s["pv_done"], KT * k + j - 2)
            nc.scalar.activation(probs[0:m, j % 3, :].rearrange("p (h c) -> p h c", h=2),
                                 st[0:m, j % 2, :, 0:HQ // 2], ACT.Exp, bias=p_scale[0:m, 0:1])\
                .then_inc(s["exps_done"], 1)

        def act_exp_hi(act, b, j):
            m = tile_keys(j)
            nc.scalar.activation(p_hi[0:m, j % 3, :].rearrange("p (h c) -> p h c", h=2),
                                 st[0:m, j % 2, :, 0:HQ // 2], ACT.Exp, bias=p_scale[0:m, 0:1])\
                .then_inc(s["p_hi_done"], 1)

        ACT_SLOT = {"K": act_k_hi, "T": act_ctx, "V": act_v, "M": act_max_row,
                    "Q": act_q_hi, "A": lambda act, b, c: act_attn(act, b)}

        def act_unit(act, b, steps=range(KT)):
            k, u = b
            for j in steps:
                for slot in STEPS[j]:
                    if slot and slot[0] in "A" and present(slot, k):
                        ACT_SLOT[slot[0]](act, b, slot[1])
                if attends(k):
                    act_exp(act, b, j)
                for slot in STEPS[j]:
                    if slot and slot[0] in "TVKQM" and present(slot, k):
                        ACT_SLOT[slot[0]](act, b, slot[1])
                if attends(k) and j not in CAST:
                    act_exp_hi(act, b, j)

        def dve_mask_max(dve, b, h):
            k, u = b
            if h == 0:
                dve.wait_ge(mask_loaded[u], 16 * turn(k + 2, u))
            nc.vector.tensor_reduce(mask_abs[mr, h:h + 1], mask_raw[mr, u, h * NK // 2:(h + 1) * NK // 2], AX.X,
                                    ALU.max, apply_absolute_value=True).then_inc(s["mask_abs_done"], 1)

        def dve_any(dve, b):
            k, u = b
            dve.wait_ge(s["mask_abs_done"], 2 * (k + 3))
            if not known(k, -1):
                dve.wait_ge(s["q_blanked"], 2 * (k + 2))
            nc.vector.tensor_scalar(any_key[mr, :], mask_abs[mr, 0:1], mask_abs[mr, 1:2], 0.0,
                                    ALU.max, ALU.is_gt).then_inc(s["any_done"], 1)
            dve.wait_ge(s["any_done"], k + 3)
            nc.vector.tensor_scalar(fill[mr, :], any_key[mr, :], -BIG, None, ALU.mult).then_inc(s["fill_done"], 1)

        def dve_mask(dve, b):
            k, u = b
            dve.wait_ge(s["fill_done"], k + 3)
            if not known(k, -1):
                for x in keys_placed:
                    dve.wait_ge(x, 96 * (k + 2))
            nc.vector.tensor_scalar(mask_add[mr, :], mask_raw[mr, u, :], 0.0, fill[mr, 0:1],
                                    ALU.is_equal, ALU.mult).then_inc(s["mask_ready"], 1)

        def dve_k_lo(dve, b, c):
            k, u = b
            dve.wait_ge(s["k_hi_stored"], NCH * (k + 2) + c + 1)
            w = chunk(c).stop - c * CH
            nc.vector.scalar_tensor_tensor(out=k_lo[:, chunk(c)], in0=ring[:, RING[("K", c)], 0:w],
                                           scalar=k_bias[:, 0:1], in1=k_hi[:, chunk(c)],
                                           op0=ALU.add, op1=ALU.subtract).then_inc(s["k_lo_stored"], 1)

        def dve_v_lo(dve, b, c):
            k, u = b
            dve.wait_ge(s["v_hi_stored"], NCH * (k + 1) + c + 1)
            for src, dst in v_parts(b, c):
                op = nc.vector.scalar_tensor_tensor(out=dst[:, :, DH:2 * DH], in0=src, scalar=V_SCALE,
                                                    in1=dst[:, :, 0:DH], op0=ALU.mult, op1=ALU.subtract)
            op.then_inc(s["v_stored"], 1)

        def dve_q(dve, b, g):
            k, u = b
            dve.wait_ge(s["q_hi_done"], 2 * (k + 2) + g + 1)
            if g == 0 and not known(k, -1):
                dve.wait_ge(s["q_moved"], k + 2)
            nc.vector.tensor_tensor(q_stage[0:64, 4 * g:4 * g + 4, :, :].rearrange("r p h q -> r (p h q)"),
                                    ring[0:64, RING[("Q", g)], 0:4 * QW], q_hi[:, g, :],
                                    ALU.subtract).then_inc(s["q_built"], 1)

        def dve_move_q(dve, b):
            k, u = b
            dve.wait_ge(s["q_built"], 2 * (k + 2))
            if not known(k, 1):
                dve.wait_ge(s["st_made"], KT * k)
            nc.vector.tensor_copy(qrs[0:ROWS, 1 - u, :, :, :].rearrange("r p h q -> r (p h q)"),
                                  q_stage[0:ROWS, :, :, :].rearrange("r p h q -> r (p h q)"))\
                .then_inc(s["q_moved"], 1)

        def dve_max(dve, b, m):
            k, u = b
            c, p = divmod(m, PAIRS)
            w = chunk(c).stop - c * CH
            dve.wait_ge(s["scored"], PAIRS * NCH * (k + 1) + m + 1)
            nc.vector.tensor_reduce(max_part[:, p, c:c + 1], ring[0:QW, RING[("S", m)], 0:w], AX.X,
                                    ALU.max).then_inc(s["max_read"], 1)

        def dve_merge_max(dve, b):
            k, u = b
            dve.wait_ge(s["max_read"], PAIRS * NCH * (k + 2))
            if not known(k, 0):
                dve.wait_ge(s["max_turned"], 2 * (k + 1))
            nc.vector.tensor_reduce(neg_max[:, :], max_part[:, :, :], AX.X, ALU.max,
                                    negate=True).then_inc(s["max_merged"], 1)

        def dve_norm(dve, b):
            k, u = b
            dve.wait_ge(s["pv_done"], KT * k)
            nc.vector.reciprocal(recip[:, :], pv_win[:, :, WIN - 1, VW - 1:VW]).then_inc(s["recip_done"], 1)
            nc.vector.tensor_reduce(pv_sum[:, :, :].rearrange("p n w -> p (n w)"),
                                    pv_win[:, :, :, 0:2 * DH].rearrange("p t h (v w) -> p (t h) w v", v=2),
                                    AX.X, ALU.add).then_inc(s["sums_read"], 1)
            dve.wait_ge(s["recip_done"], k)
            dve.wait_ge(s["sums_read"], k)
            nc.vector.tensor_tensor(normed[:, :, :].rearrange("p t (h w) -> p t h w", h=WIN),
                                    pv_sum[:, :, :].rearrange("p (t h) w -> p t h w", t=RT),
                                    recip[:, :].unsqueeze(2).unsqueeze(3).to_broadcast([P, RT, WIN, DH]),
                                    ALU.mult).then_inc(s["normed_done"], 1)

        def dve_cast(dve, b, j):
            k, u = b
            m = tile_keys(j)
            dve.wait_ge(s["exps_done"], KT * k + j + 1)
            nc.vector.tensor_copy(p_hi[0:m, j % 3, :], probs[0:m, j % 3, :]).then_inc(s["p_hi_cast"], 1)

        DVE_SLOT = {"K": dve_k_lo, "S": dve_max, "V": dve_v_lo, "Q": dve_q}

        MAXIMA_FIRST = (8,)
        BEFORE = {0: 0}
        MASK_MAX_STEPS, ANY_STEP, MASK_STEP, BLOCKS_STEP = (0, 0), 2, 4, 3

        def dve_unit(dve, b, steps=range(KT)):
            k, u = b
            if present(("V", 0), k):
                dve_move_q(dve, b)
            for j in steps:
                if j == 2 and present(("A", 0), k):
                    dve_norm(dve, b)
                order = [x for x in STEPS[j] if x and x[0] in DVE_SLOT and present(x, k)]
                if j in MAXIMA_FIRST:
                    order = [x for x in order if x[0] == "S"] + [x for x in order if x[0] != "S"]
                for slot in order[:BEFORE.get(j)]:
                    DVE_SLOT[slot[0]](dve, b, slot[1])
                if known(k, -1) and j == 0:
                    dve.wait_ge(s["blocks_zeroed"], 1)
                    for h in range(2):
                        dve_mask_max(dve, b, h)
                    dve_any(dve, b)
                    dve_mask(dve, b)
                elif present(("K", 0), k) and not known(k, -1):
                    for h in range(2):
                        if j == MASK_MAX_STEPS[h]:
                            dve_mask_max(dve, b, h)
                    if j == ANY_STEP:
                        dve_any(dve, b)
                    if j == MASK_STEP:
                        dve_mask(dve, b)
                for slot in order[BEFORE.get(j, len(order)):]:
                    DVE_SLOT[slot[0]](dve, b, slot[1])
                if j == KT - 1 and present(("S", 0), k):
                    dve_merge_max(dve, b)
                if j - 1 in CAST and attends(k):
                    dve_cast(dve, b, j - 1)

        def pool_blocks(pool, b):
            k, u = b
            pool.wait_ge(s["normed_done"], k)
            for t in range(RT):
                op = nc.gpsimd.tensor_tensor(blocks[:, t, DH * H0[t]:DH * (H0[t] + WIN)], normed[:, t, :],
                                             own[:, t, :], ALU.mult)
            op.then_inc(s["blocks_done"], 1)

        QUERY_STEP = Q_STEP - 2

        def pool_query(pool, b):
            k, u = b
            pool.wait_ge(s["any_done"], k + 3)
            if not known(k, -1):
                pool.wait_ge(s["q_spread"], 2 * (k + 2))
            if attends(k):
                pool.wait_ge(s["p_lo_done"], KT * k + QUERY_STEP)
            for h in range(2):
                nc.gpsimd.tensor_tensor(q_any[mr, :, h, :, h * DH:(h + 1) * DH],
                                        q_all[mr, bass.ds(k + 2, 1), :].rearrange("q b (p d) -> q (b p) d", p=PAIRS)
                                        [:, :, h * DH:(h + 1) * DH].unsqueeze(2).to_broadcast([NR, PAIRS, 4, DH]),
                                        any_key[mr, 0:1].unsqueeze(2).unsqueeze(3).to_broadcast([NR, PAIRS, 4, DH]),
                                        ALU.mult).then_inc(s["q_blanked"], 1)

        def pool_p_lo(pool, b, j):
            k, u = b
            m = tile_keys(j)
            if j == QUERY_STEP and present(("Q", 0), k):
                pool.wait_ge(s["q_blanked"], 2 * (k + 3))
            if j in CAST:
                pool.wait_ge(s["p_hi_cast"], len(CAST) * k + hi_count(j, True))
            else:
                pool.wait_ge(s["p_hi_done"], (KT - len(CAST)) * k + hi_count(j, False))
            nc.gpsimd.tensor_tensor(p_lo[0:m, j % 3, :], probs[0:m, j % 3, :], p_hi[0:m, j % 3, :],
                                    ALU.subtract).then_inc(s["p_lo_done"], 1)

        def pool_unit(pool, b, steps=range(KT)):
            k, u = b
            for j in steps:
                if j == QUERY_STEP and present(("Q", 0), k):
                    pool_query(pool, b)
                if attends(k):
                    pool_p_lo(pool, b, j)
                if j == BLOCKS_STEP and present(("A", 0), k):
                    pool_blocks(pool, b)

        def units(eng, unit, setup={}):
            if not setup:
                unit(eng, (-2, 0))
            for j in range(KT if setup else 0):
                if j in setup:
                    setup[j]()
                unit(eng, (-2, 0), [j])
            for k in (-1, 0):
                unit(eng, (k, k % 2))
            with eng.Fori(1, B - 4, 2) as i:
                for v in range(2):
                    unit(eng, (eng.snap(i + v), 1 - v))
            for k in (B - 3, B - 2, B - 1):
                unit(eng, (k, k % 2))

        mix_banks = [ring[:, 0, :], ring[:, 1, :]]
        xn_banks = [ring[:, 2, :], pv[:, :]]
        TILES = [range(0, 4), range(4, TT)]

        def sp_expert(sp, e, v):
            if e >= 2:
                sp.wait_ge(s["up_split"], e - 1)
            sp.dma_start(up_w[:, v, :], d["up_w"][bass.ds(e, 1), :, :].rearrange("e k i -> k (e i)"))\
                .then_inc(up_loaded[v], 16)
            if e >= 2:
                sp.wait_ge(s["down_split"], e - 1)
            sp.dma_start(down_w[:, v, :, :],
                         d["down_w"][bass.ds(e, 1), :, :].rearrange("e (c i) h -> i (e c) h", c=HC))\
                .then_inc(down_loaded[v], 16)

        def sp_route(sp, e, v):
            if e >= 3:
                sp.wait_ge(s["weighted"], HC * (e - 1))
            sp.dma_start(w_all[:, v, :], route_dram[e].unsqueeze(0).to_broadcast([P, TOK]))\
                .then_inc(w_all_loaded[v], 16)

        def dve_split(dve, e, v, raw, parts, loaded, used, hi_split, split):
            dve.wait_ge(loaded[v], 8 * turn(e, v))
            if not isinstance(e, int) or e >= 2:
                dve.wait_ge(used, HC * (e - 1))
            nc.vector.tensor_scalar(parts[:, v, 0, :], raw, W_SCALE, None, ALU.mult).then_inc(hi_split, 1)
            dve.wait_ge(hi_split, e + 1)
            nc.vector.scalar_tensor_tensor(out=parts[:, v, 1, :], in0=raw, scalar=W_SCALE, in1=parts[:, v, 0, :],
                                           op0=ALU.mult, op1=ALU.subtract).then_inc(split, 1)

        def dve_split_up(dve, e, v):
            dve_split(dve, e, v, up_w[:, v, :], up_p, up_loaded, s["up_made"], s["up_hi_split"], s["up_split"])

        def dve_split_down(dve, e, v):
            dve_split(dve, e, v, down_w[:, v, :, :].rearrange("p c h -> p (c h)"), down_p, down_loaded,
                      s["down_made"], s["down_hi_split"], s["down_split"])

        def pe_up(pe, e, v, c):
            if c == 0:
                pe.wait_ge(s["up_split"], e + 1)
            if not isinstance(e, int) or e >= 1 or c >= 2:
                pe.wait_ge(s["gelu_done"], HC * e + c - 1)
            for n, (w, x) in enumerate(((0, 0), (0, 1), (1, 0))):
                for h in range(2):
                    mm = nc.tensor.matmul(st[:, c % 2, h, 0:HALF], up_p[:, v, w, c * P:(c + 1) * P],
                                          xn_p[:, x, h * HALF:(h + 1) * HALF], start=(n == 0), stop=(n == 2))
            mm.then_inc(s["up_made"], 1)

        def act_gelu(act, e, v, c):
            act.wait_ge(s["up_made"], HC * e + c + 1)
            if not isinstance(e, int) or e >= 1:
                act.wait_ge(s["hid_lo_done"], HC * (e - 1) + c + 1)
            nc.scalar.activation(hid_raw[c].rearrange("p (h t) -> p h t", h=2), st[:, c % 2, :, 0:HALF],
                                 ACT.Gelu, bias=up_bias[:, bass.ds(e * HC + c, 1)],
                                 scale=1 / W_SCALE).then_inc(s["gelu_done"], 1)

        def dve_weight(dve, e, v, c):
            dve.wait_ge(s["gelu_done"], HC * e + c + 1)
            if isinstance(e, int) and e == 0:
                nc.vector.tensor_scalar(hid_raw[c], hid_raw[c], H_SCALE, None,
                                        ALU.mult).then_inc(s["weighted"], 1)
                return
            if c == 0:
                dve.wait_ge(w_all_loaded[v], 8 * (e + v))
            nc.vector.scalar_tensor_tensor(out=hid_raw[c], in0=hid_raw[c], scalar=H_SCALE,
                                           in1=w_all[:, v, :], op0=ALU.mult, op1=ALU.mult).then_inc(s["weighted"], 1)

        def dve_expert(dve, e, v):
            last = isinstance(e, int) and e == NE - 1
            for c in range(HC):
                dve_weight(dve, e, v, c)
                if c == 1 and not last:
                    dve_split_up(dve, e + 1 if isinstance(e, int) else dve.snap(e + 1), 1 - v)
                if c == 3 and not last:
                    dve_split_down(dve, e + 1 if isinstance(e, int) else dve.snap(e + 1), 1 - v)

        def act_expert(act, e, v):
            before = e - 1 if isinstance(e, int) else act.snap(e - 1)
            for c in range(HC):
                act_gelu(act, e, v, c)
                if c > 0:
                    act_hid_hi(act, e, v, c - 1)
                elif not known(e, 1):
                    act_hid_hi(act, before, 1 - v, HC - 1)

        def act_hid_hi(act, e, v, c):
            act.wait_ge(s["weighted"], HC * e + c + 1)
            if not isinstance(e, int) or e >= 2:
                act.wait_ge(s["down_made"], HC * (e - 2) + c + 1)
            nc.scalar.activation(hid[:, v, 0, c, :], hid_raw[c], ACT.Copy).then_inc(s["hid_hi_done"], 1)

        def pool_hid_lo(pool, e, v, c):
            pool.wait_ge(s["hid_hi_done"], HC * e + c + 1)
            nc.gpsimd.tensor_tensor(hid[:, v, 1, c, :], hid_raw[c], hid[:, v, 0, c, :],
                                    ALU.subtract).then_inc(s["hid_lo_done"], 1)

        def pe_down(pe, e, v, c):
            pe.wait_ge(s["hid_lo_done"], HC * e + c + 1)
            if c == 0:
                pe.wait_ge(s["down_split"], e + 1)
            for n, (w, x) in enumerate(((0, 0), (0, 1), (1, 0))):
                for h in range(2):
                    mm = nc.tensor.matmul(mix_banks[h][:, 0:HALF], down_p[:, v, w, c * P:(c + 1) * P],
                                          hid[:, v, x, c, h * HALF:(h + 1) * HALF],
                                          start=(isinstance(e, int) and e == 0 and c == 0 and n == 0), stop=False,
                                          skip_group_check=True)
            mm.then_inc(s["down_made"], 1)

        turned = [pv[:, :], st[:, 1, 1, :]]

        def dve_layer_norm(dve, stats, var, normed_tiles):
            for t in range(TT):
                nc.vector.bn_stats(ln_stat[:, t, :], x_tok[:, t, :]).then_inc(stats, 1)
            for t in range(TT):
                dve.wait_ge(stats, TT + t)
                nc.vector.bn_aggr(ln_mv[:, t, :], ln_stat[:, t, :]).then_inc(stats, 1)
            dve.wait_ge(stats, 2 * TT)
            nc.vector.tensor_scalar(ln_rstd[:, :], ln_mv[:, :, 1:2].rearrange("p t o -> p (t o)"), EPS, None,
                                    ALU.add).then_inc(stats, 1)
            dve.wait_ge(var, 1)
            nc.vector.reciprocal(ln_rstd[:, :], ln_rstd[:, :]).then_inc(stats, 1)
            dve.wait_ge(stats, 2 * TT + 2)
            for t in range(TT):
                nc.vector.tensor_scalar(xn[:, t, :], x_tok[:, t, :], ln_mv[:, t, 0:1], ln_rstd[:, t:t + 1],
                                        ALU.subtract, ALU.mult).then_inc(normed_tiles, 1)

        @block.sync
        def _(sp):
            sp.dma_start(x_tok[:, :, :], d["x"].rearrange("b q d -> (b q) d").rearrange("(t p) d -> p t d", p=P))\
                .then_inc(s["x_loaded"], 16)
            for i, w in enumerate(("qw", "kw", "vw", "ow")):
                sp.dma_start(w_raw[:, i, :], d[w]).then_inc(s["weights_loaded"], 16)
            sp.dma_start(ident[:, :], d["c_ident"]).then_inc(s["weights_loaded"], 16)
            sp_load_batch(sp, (0, 0))
            sp.dma_start(q_bias[mr, :], d["qb"].unsqueeze(0).to_broadcast([NR, D])).then_inc(s["consts_loaded"], 16)
            sp.dma_start(k_bias[:, :], d["kb"].unsqueeze(1)).then_inc(s["consts_loaded"], 16)
            sp.dma_start(v_bias[:, :], d["vb"].unsqueeze(1)).then_inc(s["consts_loaded"], 16)
            sp.dma_start(q_stage[mr, :, :, :].rearrange("r p h q -> r (p h q)"), d["c_onehot"])\
                .then_inc(s["consts_loaded"], 16)
            sp.dma_start(skip[mr, :], d["c_skip"]).then_inc(s["weights_loaded"], 16)
            sp.dma_start(pick[:, :, :], d["c_pick"]).then_inc(s["consts_loaded"], 16)
            sp.dma_start(own[:, :, :], d["c_own"]).then_inc(s["consts_loaded"], 16)
            sp_load_batch(sp, (1, 1))
            sp.dma_start(o_bias[:, :], d["ob"].unsqueeze(0).to_broadcast([P, D])).then_inc(s["ffn_consts"], 16)
            sp.dma_start(gate_w[:, :], d["gate_w"]).then_inc(s["ffn_consts"], 16)
            sp.dma_start(gate_b[:, :], d["gate_b"].unsqueeze(0).to_broadcast([P, E])).then_inc(s["ffn_consts"], 16)
            sp.dma_start(up_b_raw[:, :], d["up_b"].rearrange("e (c i) -> (e c) i", c=HC)).then_inc(s["ffn_consts"], 16)
            sp.dma_start(down_b[:, :], d["down_b"]).then_inc(s["ffn_consts"], 16)
            sp.dma_start(rank[:, :], d["c_rank"]).then_inc(s["ffn_consts"], 16)
            sp.dma_start(gates[:, 0:1], d["gx"].unsqueeze(0).to_broadcast([P, 1])).then_inc(s["ffn_consts"], 16)
            sp.dma_start(gates[:, 1:2], d["gf"].unsqueeze(0).to_broadcast([P, 1])).then_inc(s["ffn_consts"], 16)
            sp_expert(sp, 0, 0)
            sp_expert(sp, 1, 1)

            units(sp, sp_unit)
            sp_expert(sp, 2, 0)
            sp.wait_ge(s["route_copied"], 2)
            sp.dma_start(route_dram[:, :], routeT[:, :]).then_inc(s["route_stored"], 16)
            sp.wait_ge(s["route_stored"], 16)
            sp_route(sp, 1, 1)
            sp_route(sp, 2, 0)
            for e in range(3, NE):
                sp_expert(sp, e, e % 2)
                sp_route(sp, e, e % 2)
            x_out = out.rearrange("b q d -> (b q) d").rearrange("(t p) d -> p t d", p=P)
            for h in range(2):
                sp.wait_ge(s["out_ready"], h + 1)
                t0, t1 = TILES[h][0], TILES[h][-1] + 1
                sp.dma_start(x_out[:, t0:t1, :], acc[:, t0:t1, :]).then_inc(s["out_stored"], 16)
            sp.wait_ge(s["out_stored"], 32)

        NFFN = 8
        NCONST = 6

        @block.scalar
        def _(act):
            act.wait_ge(s["ln_stats"], 2 * TT + 1)
            nc.scalar.activation(ln_rstd[:, :], ln_rstd[:, :], ACT.Sqrt).then_inc(s["ln_var"], 1)
            act.wait_ge(s["w_turned"], 1)
            nc.scalar.activation(w_t[:, :, :].rearrange("p i d -> p (i d)"), pv[:, :],
                                 ACT.Copy).then_inc(s["w_copied"], 1)
            act.wait_ge(s["consts_loaded"], 16 * NCONST)

            def keep_turned():
                for g in range(2):
                    act.wait_ge(s["ln_turned"], g + 1)
                    src = turned[g][:, 0:HALF].rearrange("p (b q) -> p b q", q=S)
                    dst = lnT[:, 8 * g * NR:8 * (g + 1) * NR].rearrange("p (b r) -> p b r", r=NR)
                    for cols, rows in ((slice(0, QSPLIT), slice(0, QSPLIT)), (slice(QSPLIT, S), slice(QSPLIT + 1, NR))):
                        nc.scalar.activation(dst[:, :, rows], src[:, :, cols], ACT.Copy).then_inc(s["ln_copied"], 1)

            act.wait_ge(s["ones_set"], 4)
            units(act, act_unit, {0: keep_turned})
            act_attn(act, (B, 0))

            act.wait_ge(s["ffn_consts"], 16 * NFFN)
            nc.scalar.activation(tanh_g[:, :], gates[:, :], ACT.Tanh).then_inc(s["gates_tanh"], 1)
            act.wait_ge(s["ffn_stats"], 2 * TT + 1)
            nc.scalar.activation(ln_rstd[:, :], ln_rstd[:, :], ACT.Sqrt).then_inc(s["ffn_var"], 1)
            for h in range(2):
                w = P * len(TILES[h])
                act.wait_ge(s["xn_turned"], h + 1)
                nc.scalar.activation(xnT[:, 4 * P * h:4 * P * h + w], xn_banks[h][:, 0:w],
                                     ACT.Copy).then_inc(s["xn_copied"], 1)
                nc.scalar.activation(xn_p[:, 0, 4 * P * h:4 * P * h + w], xn_banks[h][:, 0:w],
                                     ACT.Copy).then_inc(s["xn_hi_done"], 1)
            act.wait_ge(s["bias_turned"], 1)
            nc.scalar.activation(up_bias[:, :], ring[:, 0, 0:NE * HC], ACT.Copy).then_inc(s["bias_copied"], 1)
            act.wait_ge(s["score_raw"], 1)
            nc.scalar.activation(score[:, :, :], score[:, :, :], ACT.Sigmoid).then_inc(s["score_done"], 1)
            act.wait_ge(s["bias_copied"], 1)
            act_expert(act, 0, 0)
            for h in range(2):
                w = P * len(TILES[h])
                act.wait_ge(s["route_turned"], h + 1)
                nc.scalar.activation(routeT[:, 4 * P * h:4 * P * h + w], xn_banks[h][0:NE, 0:w],
                                     ACT.Copy).then_inc(s["route_copied"], 1)
            act_expert(act, 1, 1)
            act_expert(act, 2, 0)
            with act.Fori(3, NE - 1, 2) as i:
                for v in (1, 0):
                    act_expert(act, act.snap(i + 1 - v), v)
            act_hid_hi(act, NE - 1, 0, HC - 1)
            act.wait_ge(s["mixed"], 1)
            nc.scalar.activation(xnT[:, 0:HALF], mix_banks[0][:, 0:HALF], ACT.Copy,
                                 scale=1 / (W_SCALE * H_SCALE)).then_inc(s["mix_copied"], 1)

        @block.tensor
        def _(pe):
            pe.wait_ge(s["weights_loaded"], 96)
            for i in range(4):
                mm = nc.tensor.transpose(pv[:, i * P:(i + 1) * P], w_raw[:, i, :], ident[:, :])
            mm.then_inc(s["w_turned"], 1)
            pe.wait_ge(s["w_copied"], 1)

            def turn_queries():
                for g in range(2):
                    pe.wait_ge(s["ln_done"], (TT + 1) // 2 if g == 0 else TT)
                    for t in range(TT):
                        lo, hi = max(t * P, g * HALF), min((t + 1) * P, (g + 1) * HALF)
                        if lo < hi:
                            rows = slice(lo - t * P, hi - t * P)
                            mm = nc.tensor.matmul(turned[g][:, lo - g * HALF:hi - g * HALF], xn[rows, t, :],
                                                  ident[rows, rows], start=True, stop=True)
                    mm.then_inc(s["ln_turned"], 1)

            def make_queries():
                pe.wait_ge(s["ln_gap"], 1)
                for g in range(4):
                    pe.wait_ge(s["ln_copied"], 2 if g < 2 else 4)
                    for i in range(4):
                        b = 4 * g + i
                        mm = nc.tensor.matmul(st[mr, g // 2, g % 2, i * D:(i + 1) * D],
                                              lnT[:, b * NR:(b + 1) * NR], w_t[:, 0, :], start=True, stop=True)
                    mm.then_inc(s["q_made"], 1)

            def await_ones():
                pe.wait_ge(s["ones_placed"], 16)

            units(pe, pe_unit, {0: turn_queries, K_STEP: make_queries, KT - 1: await_ones})
            for j in range(KT - LAG, KT):
                pe_pv(pe, (B - 1, 1), j)
            pe_attn(pe, (B, 0))

            pe.wait_ge(s["attn_stored"], B)
            for h in range(2):
                for i, t in enumerate(TILES[h]):
                    mm = nc.tensor.matmul(mix_banks[h][:, i * P:(i + 1) * P], attnT[:, t * P:(t + 1) * P],
                                          w_t[:, 3, :], start=True, stop=True)
                mm.then_inc(s["projected"], 1)
            for h in range(2):
                for i, t in enumerate(TILES[h]):
                    pe.wait_ge(s["ffn_ln_done"], t + 1)
                    if h == 1:
                        pe.wait_ge(s["normed_done"], B)
                    mm = nc.tensor.transpose(xn_banks[h][:, i * P:(i + 1) * P], xn[:, t, :], ident[:, :])
                mm.then_inc(s["xn_turned"], 1)
            pe.wait_ge(s["x1_step"], 2)
            pe.wait_ge(s["ffn_consts"], 16 * NFFN)
            nc.tensor.transpose(ring[:, 0, 0:NE * HC], up_b_raw[:, :], ident[0:NE * HC, 0:NE * HC])\
                .then_inc(s["bias_turned"], 1)
            pe.wait_ge(s["xn_copied"], 2)
            for t in range(TT):
                mm = nc.tensor.matmul(ring[:, 1, t * E:(t + 1) * E], xnT[:, t * P:(t + 1) * P], gate_w[:, :],
                                      start=True, stop=True)
            mm.then_inc(s["gate_made"], 1)
            pe.wait_ge(s["xn_split"], 2)
            for c in range(HC):
                pe_up(pe, 0, 0, c)
            pe.wait_ge(s["route_done"], 1)
            for h in range(2):
                for i, t in enumerate(TILES[h]):
                    mm = nc.tensor.transpose(xn_banks[h][0:NE, i * P:(i + 1) * P], route[:, :, t], ident[:, :])
                mm.then_inc(s["route_turned"], 1)
            pe.wait_ge(s["bias_copied"], 1)
            for c in range(HC):
                pe_up(pe, 1, 1, c)
                pe_down(pe, 0, 0, c)
            with pe.Fori(2, NE - 2, 2) as i:
                for v in range(2):
                    e = pe.snap(i + v)
                    for c in range(HC):
                        pe_up(pe, e, v, c)
                        pe_down(pe, pe.snap(e - 1), 1 - v, c)
            for c in range(HC):
                pe_up(pe, NE - 1, 0, c)
                pe_down(pe, NE - 2, 1, c)
            for c in range(HC):
                pe_down(pe, NE - 1, 0, c)
            pe.wait_ge(s["route_copied"], 2)
            pe.wait_ge(s["down_b_scaled"], 1)
            for h in range(2):
                nc.tensor.matmul(mix_banks[h][:, 0:HALF], down_bs[:, :], routeT[:, h * HALF:(h + 1) * HALF],
                                 start=False, stop=True, skip_group_check=True).then_inc(s["mixed"], 1)
            for h in range(2):
                pe.wait_ge(s["mix_copied"], 2)
                for i, t in enumerate(TILES[h]):
                    mm = nc.tensor.transpose(st[:, 0, h, i * P:(i + 1) * P], xnT[:, t * P:(t + 1) * P], ident[:, :])
                mm.then_inc(s["mix_turned"], 1)

        @block.vector
        def _(dve):
            nc.vector.memset(p_scale[:, :], float(np.log(P_SCALE))).then_inc(s["ones_set"], 1)
            nc.vector.memset(lo_row[0:32, :], 0.0).then_inc(s["ones_set"], 1)
            nc.vector.memset(lo_row[32:64, :], 1.0).then_inc(s["ones_set"], 1)
            nc.vector.memset(ones_row[:, :], 1.0).then_inc(s["ones_set"], 1)
            nc.vector.memset(v_ext[:, :, :, :, VW - 1:VW], 1.0).then_inc(s["dve_step"], 1)
            nc.vector.memset(lnT[:, :].rearrange("p (b r) -> p b r", r=NR)[:, :, QSPLIT:QSPLIT + 1], 0.0)\
                .then_inc(s["ln_gap"], 1)
            dve.wait_ge(s["x_loaded"], 16)
            dve_layer_norm(dve, s["ln_stats"], s["ln_var"], s["ln_done"])
            dve.wait_ge(s["consts_loaded"], 16 * NCONST)

            def store_queries():
                for g in range(4):
                    dve.wait_ge(s["q_made"], g + 1)
                    nc.vector.tensor_tensor(q_all[mr, 4 * g:4 * g + 4, :],
                                            st[mr, g // 2, g % 2, :].rearrange("q (b d) -> q b d", b=4),
                                            q_bias[mr, :].unsqueeze(1).to_broadcast([NR, 4, D]), ALU.add)\
                        .then_inc(s["dve_step"], 1)
                dve.wait_ge(s["dve_step"], 5)
                nc.vector.tensor_scalar(q_all[mr, :, :], q_all[mr, :, :], float(DH) ** -0.5, None,
                                        ALU.mult).then_inc(s["q_stored"], 1)

            units(dve, dve_unit, {K_STEP: store_queries})
            dve_norm(dve, (B, 0))

            for e in range(2):
                dve_split_up(dve, e, e)
                dve_split_down(dve, e, e)
            dve.wait_ge(s["gates_tanh"], 1)
            for h in range(2):
                t0, t1 = TILES[h][0], TILES[h][-1] + 1
                dve.wait_ge(s["projected"], h + 1)
                nc.vector.tensor_tensor(xn[:, t0:t1, :],
                                        mix_banks[h][:, 0:(t1 - t0) * P].rearrange("p (t d) -> p t d", d=D),
                                        o_bias[:, :].unsqueeze(1).to_broadcast([P, t1 - t0, D]),
                                        ALU.add).then_inc(s["x1_step"], 1)
            for h in range(2):
                t0, t1 = TILES[h][0], TILES[h][-1] + 1
                dve.wait_ge(s["x1_step"], h + 1)
                nc.vector.scalar_tensor_tensor(out=x_tok[:, t0:t1, :], in0=xn[:, t0:t1, :], scalar=tanh_g[:, 0:1],
                                               in1=x_tok[:, t0:t1, :], op0=ALU.mult,
                                               op1=ALU.add).then_inc(s["x1_done"], 1)
            dve.wait_ge(s["x1_done"], 2)
            dve_layer_norm(dve, s["ffn_stats"], s["ffn_var"], s["ffn_ln_done"])
            for h in range(2):
                cols = slice(4 * P * h, 4 * P * h + P * len(TILES[h]))
                dve.wait_ge(s["xn_hi_done"], h + 1)
                nc.vector.tensor_tensor(xn_p[:, 1, cols], xn_banks[h][:, 0:P * len(TILES[h])], xn_p[:, 0, cols],
                                        ALU.subtract).then_inc(s["xn_split"], 1)
            nc.vector.tensor_scalar(down_bs[:, :], down_b[:, :], W_SCALE * H_SCALE, None,
                                    ALU.mult).then_inc(s["down_b_scaled"], 1)

            dve.wait_ge(s["gate_made"], 1)
            nc.vector.tensor_tensor(score[:, :, :], ring[:, 1, 0:TT * E].rearrange("p (t e) -> p t e", e=E),
                                    gate_b[:, :].unsqueeze(1).to_broadcast([P, TT, E]),
                                    ALU.add).then_inc(s["score_raw"], 1)
            dve.wait_ge(s["score_done"], 1)
            steps = [0]

            def then(op):
                op.then_inc(s["route_step"], 1)
                steps[0] += 1
                dve.wait_ge(s["route_step"], steps[0])

            def over_experts(v):
                return v.unsqueeze(2).to_broadcast([P, TT, E])

            rank3 = rank[:, :].rearrange("p (t e) -> p t e", e=E)
            then(nc.vector.memset(route[:, 0, :], 1.0))
            for r, chosen in enumerate((pick1, pick2)):
                then(nc.vector.tensor_reduce(topv[:, r, :], score[:, :, :], AX.X, ALU.max))
                then(nc.vector.tensor_tensor(tmp[:, :, :], score[:, :, :], over_experts(topv[:, r, :]), ALU.is_equal))
                then(nc.vector.tensor_tensor(tmp[:, :, :], tmp[:, :, :], rank3, ALU.mult))
                then(nc.vector.tensor_reduce(tmpv[:, :], tmp[:, :, :], AX.X, ALU.max))
                then(nc.vector.tensor_tensor(chosen[:, :, :], tmp[:, :, :], over_experts(tmpv[:, :]), ALU.is_equal))
                dve_weight(dve, 0, 0, r)
                if r == 0:
                    then(nc.vector.scalar_tensor_tensor(out=score[:, :, :], in0=chosen[:, :, :], scalar=-4.0,
                                                        in1=score[:, :, :], op0=ALU.mult, op1=ALU.add))
            then(nc.vector.scalar_tensor_tensor(out=tmpv[:, :], in0=topv[:, 0, :], scalar=1e-6, in1=topv[:, 1, :],
                                                op0=ALU.add, op1=ALU.add))
            then(nc.vector.reciprocal(tmpv[:, :], tmpv[:, :]))
            for r, chosen in enumerate((pick1, pick2)):
                then(nc.vector.tensor_tensor(topv[:, r, :], topv[:, r, :], tmpv[:, :], ALU.mult))
                then(nc.vector.tensor_tensor(chosen[:, :, :], chosen[:, :, :], over_experts(topv[:, r, :]), ALU.mult))
            nc.vector.tensor_tensor(route[:, 1:NE, :].rearrange("p e t -> p t e"), pick1[:, :, :], pick2[:, :, :],
                                    ALU.add).then_inc(s["route_done"], 1)
            for c in (2, 3):
                dve_weight(dve, 0, 0, c)
            with dve.Fori(1, NE - 3, 2) as i:
                for v in (1, 0):
                    dve_expert(dve, dve.snap(i + 1 - v), v)
            dve_expert(dve, NE - 2, 1)
            dve_expert(dve, NE - 1, 0)
            dve.wait_ge(s["mixed"], 2)
            nc.vector.tensor_scalar(xnT[:, HALF:TOK], mix_banks[1][:, 0:HALF], 1 / (W_SCALE * H_SCALE), None,
                                    ALU.mult).then_inc(s["mix_copied"], 1)
            for h in range(2):
                t0, t1 = TILES[h][0], TILES[h][-1] + 1
                dve.wait_ge(s["mix_turned"], h + 1)
                op = nc.vector.tensor_reduce(tmpv[:, t0:t1],
                                             st[:, 0, h, 0:(t1 - t0) * P].rearrange("p (t d) -> p t d", d=D), AX.X,
                                             ALU.max, apply_absolute_value=True)
            op.then_inc(s["out_step"], 1)
            dve.wait_ge(s["out_step"], 1)
            nc.vector.tensor_scalar(tmpv[:, :], tmpv[:, :], 0.1, 1e-6, ALU.mult, ALU.add).then_inc(s["out_step"], 1)
            dve.wait_ge(s["out_step"], 2)
            nc.vector.reciprocal(tmpv[:, :], tmpv[:, :]).then_inc(s["out_step"], 1)
            dve.wait_ge(s["out_step"], 3)
            nc.vector.tensor_scalar(tmpv[:, :], tmpv[:, :], tanh_g[:, 1:2], 0.1, ALU.mult,
                                    ALU.mult).then_inc(s["out_step"], 1)
            dve.wait_ge(s["out_step"], 4)
            for h in range(2):
                for i, t in enumerate(TILES[h]):
                    op = nc.vector.scalar_tensor_tensor(out=acc[:, t, :], in0=st[:, 0, h, i * P:(i + 1) * P],
                                                        scalar=tmpv[:, t:t + 1], in1=x_tok[:, t, :],
                                                        op0=ALU.mult, op1=ALU.add)
                op.then_inc(s["out_ready"], 1)

        @block.gpsimd
        def _(pool):
            nc.gpsimd.memset(mask_raw[ONEROW:ONEROW + 1, :, :], 1).then_inc(s["blocks_zeroed"], 1)
            pool.wait_ge(s["blocks_zeroed"], 1)
            nc.gpsimd.memset(q_any[mr, :, :, :, :], 0.0).then_inc(s["blocks_zeroed"], 1)
            pool.wait_ge(s["blocks_zeroed"], 2)
            nc.gpsimd.memset(blocks[:, :, :], 0.0).then_inc(s["blocks_zeroed"], 1)
            pool.wait_ge(s["blocks_zeroed"], 3)
            pool.wait_ge(s["consts_loaded"], 16 * NCONST)
            pool.wait_ge(s["q_stored"], 1)
            units(pool, pool_unit)
            pool_blocks(pool, (B, 0))
            for c in range(HC):
                pool_hid_lo(pool, 0, 0, c)
            with pool.Fori(1, NE - 1, 2) as i:
                for v in (1, 0):
                    e = pool.snap(i + 1 - v)
                    for c in range(HC):
                        pool_hid_lo(pool, e, v, c)


_INS = {
    "x": "x", "ctx": "ctx_1024", "mask": "mask_BxSxS2_if1", "gx": "g_xattn", "gf": "g_ffn",
    "qw": "L0_xattn_qw", "qb": "L0_xattn_qb", "kw": "L0_xattn_kw", "kb": "L0_xattn_kb",
    "vw": "L0_xattn_vw", "vb": "L0_xattn_vb", "ow": "L0_xattn_ow", "ob": "L0_xattn_ob",
    "gate_w": "L0_ffn_gate_w", "gate_b": "L0_ffn_bias",
}


def kernel(**inputs):
    import concourse.bacc as _bacc
    from concourse.bass_utils import run_bass_kernel_spmd as _run

    arrays = {k: np.ascontiguousarray(inputs[v]) for k, v in _INS.items()}
    for k, routed, shared in (("up_w", "L0_ffn_up_w", "L0_ffn_sw_up"), ("up_b", "L0_ffn_up_b", "L0_ffn_sb_up"),
                              ("down_w", "L0_ffn_down_w", "L0_ffn_sw_down"),
                              ("down_b", "L0_ffn_down_b", "L0_ffn_sb_down")):
        arrays[k] = np.concatenate([np.asarray(inputs[shared])[None], np.asarray(inputs[routed])])
    arrays.update(constants())
    nc = _bacc.Bacc("TRN2", target_bir_lowering=False, num_devices=1)
    feeds, aps = {}, {}
    for k, a in arrays.items():
        feeds["in_" + k] = a
        aps[k] = nc.dram_tensor("in_" + k, a.shape, mybir.dt.from_np(a.dtype), kind="ExternalInput").ap()
    out = nc.dram_tensor("out_0", (B, S, D), F32, kind="ExternalOutput").ap()
    flamingo_kernel(nc, aps, out)
    r = _run(nc, [feeds], core_ids=[0])
    return r.results[0]["out_0"]
```
